# Optimizing a Trainium2 kernel written in Bass

```python
import numpy as np
import jax
import jax.numpy as jnp

def _softmax(x, axis=-1):
    return jax.nn.softmax(x, axis=axis)

def _gelu(x):
    return jax.nn.gelu(x, approximate=True)

def _silu(x):
    return jax.nn.silu(x)

def _sigmoid(x):
    return jax.nn.sigmoid(x)

def _layernorm(x, axis=-1, eps=1e-05):
    m = jnp.mean(x, axis=axis, keepdims=True)
    v = jnp.var(x, axis=axis, keepdims=True)
    return (x - m) / jnp.sqrt(v + eps)

def _scatter_add(tgt, idx, src, axis=0):
    return tgt.at[idx].add(src)

def _segment_sum(src, seg, n):
    return jax.ops.segment_sum(src, seg, n)
kernel_name = 'mk_seq_postln_d1_jaxref_r8_1cb8d7'

def setup_inputs(seed: int=0):
    np.random.seed(seed)
    _w = jnp.asarray

    def _L0_attn_setup():
        import jax, jax.numpy as jnp
        import numpy as np
        B_SZ, SEQ, D_MODEL = (2, 256, 256)
        D_INNER, D_XB, INTER = (512, 128, 1024)
        HEADDIM = 64
        DSTATE = 64
        NHEADS = D_INNER // HEADDIM
        N_XB = D_XB // HEADDIM
        REP = NHEADS // N_XB
        D_IN_PROJ = D_INNER + D_XB + D_XB + D_INNER + NHEADS
        EPS = 1e-05

        def _layernorm(x, w, b):
            mu = jnp.mean(x, -1, keepdims=True)
            var = jnp.mean((x - mu) ** 2, -1, keepdims=True)
            return (x - mu) * jax.lax.rsqrt(var + EPS) * w + b

        def _mamba2(hs, W_in, dt_bias, A_log, D, norm_w, W_out):
            B, L, _ = hs.shape
            zxbcdt = hs @ W_in
            splits = [D_INNER, D_INNER + D_XB, D_INNER + 2 * D_XB, D_INNER + 2 * D_XB + D_INNER]
            z, xb, Bp, Cp, dt = jnp.split(zxbcdt, splits, axis=-1)
            xh = jnp.repeat(xb.reshape(B, L, N_XB, HEADDIM), REP, axis=2)
            Bh = jnp.repeat(Bp.reshape(B, L, N_XB, DSTATE), REP, axis=2)
            Ch = Cp.reshape(B, L, NHEADS, DSTATE)
            dt = jax.nn.softplus(dt + dt_bias)
            A = -jnp.exp(A_log)
            dA = jnp.exp(dt * A)

            def step(state, inp):
                dA_t, dt_t, B_t, x_t, C_t = inp
                dBx = (dt_t[:, :, None] * x_t)[..., None] * B_t[:, :, None, :]
                state = state * dA_t[:, :, None, None] + dBx
                y_t = jnp.einsum('bhpn,bhn->bhp', state, C_t)
                return (state, y_t)
            xs = (jnp.swapaxes(dA, 0, 1), jnp.swapaxes(dt, 0, 1), jnp.swapaxes(Bh, 0, 1), jnp.swapaxes(xh, 0, 1), jnp.swapaxes(Ch, 0, 1))
            state0 = jnp.zeros((B, NHEADS, HEADDIM, DSTATE), hs.dtype)
            _, ys = jax.lax.scan(step, state0, xs)
            y = jnp.swapaxes(ys, 0, 1) + D[None, None, :, None] * xh
            y = y.reshape(B, L, D_INNER)
            yg = y * jax.nn.silu(z)
            yn = yg * jax.lax.rsqrt(jnp.mean(yg * yg, -1, keepdims=True) + EPS) * norm_w
            return yn @ W_out
        key = jax.random.key(seed)
        ks = jax.random.split(key, 10)
        s = 0.02
        return {'hidden_states': jax.random.normal(ks[0], (B_SZ, SEQ, D_MODEL), jnp.float32), 'ln_w': jnp.ones((D_MODEL,), jnp.float32), 'ln_b': jnp.zeros((D_MODEL,), jnp.float32), 'W_in': jax.random.normal(ks[1], (D_MODEL, D_IN_PROJ), jnp.float32) * s, 'dt_bias': jax.random.uniform(ks[2], (NHEADS,), jnp.float32, -4.0, -2.0), 'A_log': jnp.log(jnp.arange(1, NHEADS + 1, dtype=jnp.float32)), 'D': jnp.ones((NHEADS,), jnp.float32), 'norm_w': jnp.ones((D_INNER,), jnp.float32), 'W_out': jax.random.normal(ks[3], (D_INNER, D_MODEL), jnp.float32) * s, 'fc1_w': jax.random.normal(ks[4], (D_MODEL, INTER), jnp.float32) * s, 'fc1_b': jnp.zeros((INTER,), jnp.float32), 'fc2_w': jax.random.normal(ks[5], (INTER, D_MODEL), jnp.float32) * s, 'fc2_b': jnp.zeros((D_MODEL,), jnp.float32)}
    _L0_attn_in = _L0_attn_setup()

    def _L0_ffn_setup():
        import jax, jax.numpy as jnp
        import numpy as np
        B, S, D, H = (8, 512, 256, 640)

        def ternarize_weight(w):
            abs_mean = jnp.maximum(jnp.mean(jnp.abs(w)), 1e-05)
            thr = 0.7 * abs_mean
            one = jnp.ones((), dtype=w.dtype)
            q = jnp.where(w > thr, one, jnp.where(w < -thr, -one, jnp.zeros((), dtype=w.dtype)))
            return w + jax.lax.stop_gradient(q * abs_mean - w)
        key = jax.random.key(seed)
        k1, k2, k3 = jax.random.split(key, 3)
        x = jax.random.normal(k1, (B, S, D), dtype=jnp.float32)
        w_fc = jax.random.normal(k2, (H, D), dtype=jnp.float32) / np.sqrt(D).astype(np.float32)
        w_proj = jax.random.normal(k3, (D, H), dtype=jnp.float32) / np.sqrt(H).astype(np.float32)
        return {'x': x, 'w_fc': w_fc, 'w_proj': w_proj}
    _L0_ffn_in = _L0_ffn_setup()
    _d = {'L0_attn_hidden_states': _L0_attn_in['hidden_states'], 'L0_attn_ln_w': _L0_attn_in['ln_w'], 'L0_attn_ln_b': _L0_attn_in['ln_b'], 'L0_attn_W_in': _L0_attn_in['W_in'], 'L0_attn_dt_bias': _L0_attn_in['dt_bias'], 'L0_attn_A_log': _L0_attn_in['A_log'], 'L0_attn_D': _L0_attn_in['D'], 'L0_attn_norm_w': _L0_attn_in['norm_w'], 'L0_attn_W_out': _L0_attn_in['W_out'], 'L0_attn_fc1_w': _L0_attn_in['fc1_w'], 'L0_attn_fc1_b': _L0_attn_in['fc1_b'], 'L0_attn_fc2_w': _L0_attn_in['fc2_w'], 'L0_attn_fc2_b': _L0_attn_in['fc2_b'], 'L0_ffn_w_fc': _L0_ffn_in['w_fc'], 'L0_ffn_w_proj': _L0_ffn_in['w_proj']}
    _x0 = _d['L0_attn_hidden_states']
    _d['L0_attn_hidden_states'] = jax.random.normal(jax.random.fold_in(jax.random.key(seed), 1), (4, 256, 256), dtype=_x0.dtype)
    del _x0
    return _d

def reference(L0_attn_hidden_states, L0_attn_ln_w, L0_attn_ln_b, L0_attn_W_in, L0_attn_dt_bias, L0_attn_A_log, L0_attn_D, L0_attn_norm_w, L0_attn_W_out, L0_attn_fc1_w, L0_attn_fc1_b, L0_attn_fc2_w, L0_attn_fc2_b, L0_ffn_w_fc, L0_ffn_w_proj):

    def _L0_attn_ref(hidden_states, ln_w, ln_b, W_in, dt_bias, A_log, D, norm_w, W_out, fc1_w, fc1_b, fc2_w, fc2_b):
        import jax, jax.numpy as jnp
        import numpy as np
        B_SZ, SEQ, D_MODEL = (2, 256, 256)
        D_INNER, D_XB, INTER = (512, 128, 1024)
        HEADDIM = 64
        DSTATE = 64
        NHEADS = D_INNER // HEADDIM
        N_XB = D_XB // HEADDIM
        REP = NHEADS // N_XB
        D_IN_PROJ = D_INNER + D_XB + D_XB + D_INNER + NHEADS
        EPS = 1e-05

        def _layernorm(x, w, b):
            mu = jnp.mean(x, -1, keepdims=True)
            var = jnp.mean((x - mu) ** 2, -1, keepdims=True)
            return (x - mu) * jax.lax.rsqrt(var + EPS) * w + b

        def _mamba2(hs, W_in, dt_bias, A_log, D, norm_w, W_out):
            B, L, _ = hs.shape
            zxbcdt = hs @ W_in
            splits = [D_INNER, D_INNER + D_XB, D_INNER + 2 * D_XB, D_INNER + 2 * D_XB + D_INNER]
            z, xb, Bp, Cp, dt = jnp.split(zxbcdt, splits, axis=-1)
            xh = jnp.repeat(xb.reshape(B, L, N_XB, HEADDIM), REP, axis=2)
            Bh = jnp.repeat(Bp.reshape(B, L, N_XB, DSTATE), REP, axis=2)
            Ch = Cp.reshape(B, L, NHEADS, DSTATE)
            dt = jax.nn.softplus(dt + dt_bias)
            A = -jnp.exp(A_log)
            dA = jnp.exp(dt * A)

            def step(state, inp):
                dA_t, dt_t, B_t, x_t, C_t = inp
                dBx = (dt_t[:, :, None] * x_t)[..., None] * B_t[:, :, None, :]
                state = state * dA_t[:, :, None, None] + dBx
                y_t = jnp.einsum('bhpn,bhn->bhp', state, C_t)
                return (state, y_t)
            xs = (jnp.swapaxes(dA, 0, 1), jnp.swapaxes(dt, 0, 1), jnp.swapaxes(Bh, 0, 1), jnp.swapaxes(xh, 0, 1), jnp.swapaxes(Ch, 0, 1))
            state0 = jnp.zeros((B, NHEADS, HEADDIM, DSTATE), hs.dtype)
            _, ys = jax.lax.scan(step, state0, xs)
            y = jnp.swapaxes(ys, 0, 1) + D[None, None, :, None] * xh
            y = y.reshape(B, L, D_INNER)
            yg = y * jax.nn.silu(z)
            yn = yg * jax.lax.rsqrt(jnp.mean(yg * yg, -1, keepdims=True) + EPS) * norm_w
            return yn @ W_out
        residual = hidden_states
        hs = _layernorm(hidden_states, ln_w, ln_b)
        attn = _mamba2(hs, W_in, dt_bias, A_log, D, norm_w, W_out)
        mlp = jax.nn.gelu(hs @ fc1_w + fc1_b, approximate=True) @ fc2_w + fc2_b
        return attn + mlp + residual

    def _L0_ffn_ref(x, w_fc, w_proj):
        import jax, jax.numpy as jnp
        import numpy as np
        B, S, D, H = (8, 512, 256, 640)

        def ternarize_weight(w):
            abs_mean = jnp.maximum(jnp.mean(jnp.abs(w)), 1e-05)
            thr = 0.7 * abs_mean
            one = jnp.ones((), dtype=w.dtype)
            q = jnp.where(w > thr, one, jnp.where(w < -thr, -one, jnp.zeros((), dtype=w.dtype)))
            return w + jax.lax.stop_gradient(q * abs_mean - w)
        h = jnp.einsum('bsd,hd->bsh', x, ternarize_weight(w_fc))
        h = jnp.square(jax.nn.relu(h))
        return jnp.einsum('bsh,dh->bsd', h, ternarize_weight(w_proj))
    x = L0_attn_hidden_states
    x = _layernorm(x + _L0_attn_ref(x, L0_attn_ln_w, L0_attn_ln_b, L0_attn_W_in, L0_attn_dt_bias, L0_attn_A_log, L0_attn_D, L0_attn_norm_w, L0_attn_W_out, L0_attn_fc1_w, L0_attn_fc1_b, L0_attn_fc2_w, L0_attn_fc2_b), axis=-1)
    x = _layernorm(x + _L0_ffn_ref(x, L0_ffn_w_fc, L0_ffn_w_proj), axis=-1)
    return x

_drawn_inputs = setup_inputs


def setup_inputs(seed=0):
    import zlib

    import numpy as np

    out = dict(_drawn_inputs(seed))
    spreads = {'L0_attn_ln_w': (1.0, 0.2),
     'L0_attn_ln_b': (0.0, 0.319),
     'L0_attn_D': (1.0, 0.6),
     'L0_attn_norm_w': (1.0, 0.2),
     'L0_attn_fc1_b': (0.0, 0.651),
     'L0_attn_fc2_b': (0.0, 0.1)}
    factors = {'L0_attn_dt_bias': 8.0, 'L0_attn_A_log': 5.887}
    for name, (base, spread) in spreads.items():
        noise = np.random.default_rng([zlib.crc32(name.encode()), seed]).standard_normal(out[name].shape)
        drawn = base * np.exp(spread * noise) if base else spread * noise
        out[name] = jnp.asarray(drawn.astype(out[name].dtype))
    for name, factor in factors.items():
        out[name] = (out[name] * factor).astype(out[name].dtype)
    return out
```

```python
import concourse.bass as bass
from concourse import mybir
from contextlib import ExitStack

P = 128
D = 256
KD = D // P
T = 1024
NT = T // P
SEQS = 4
SL = T // SEQS
HALF = T // 2
TPH = HALF // P
NH = 8
HD = 64
GROUPS = 2
REP = NH // GROUPS
DI = NH * HD
KI = DI // P
F1 = 1024
KF = F1 // P
H2 = 640
KH = H2 // P
XD = GROUPS * HD + NH
WX = XD + GROUPS * HD
EPS = 1e-5
RING = 6
FSLOTS = 3
PAIRS = REP
ESLOTS = 4
BLK = SL + P


def psum_plan():
    alloc, filled = [], []

    def tile(*name):
        alloc.append(name)
        filled.append(name)

    for h in range(2):
        if h == 0:
            tile("T", 0, 0), tile("T", 0, 1)
        for b in range(2):
            tile("XD", h, b)
        tile("BT", h)
        for i in range(PAIRS):
            tile("C", h, i)
        for t in range(TPH):
            tile("Z", h, t)
        for m in range(KF):
            tile("FC1", h, m)
        if h == 0:
            tile("AM")
        tile("CUMS", h), tile("CUMT", h)
        kind = "T" if h == 0 else "X1T"
        for b in range(2):
            tile(kind, 1 - h, b)
        for s in (2 * h, 2 * h + 1):
            for i in range(PAIRS):
                tile("CB", s, i), tile("G", s, i, 0), tile("G", s, i, 1)
            alloc += [("FW", s, 0), ("FW", s, 1), ("YT", s, 0), ("YT", s, 1)]
            filled += [("YT", s, 0), ("YT", s, 1), ("FW", s, 0), ("FW", s, 1)]
    for m in range(KH):
        tile("FF1", 0, m)
    for b in range(2):
        tile("X1T", 1, b)
    for t in range(TPH):
        tile("FF2", 0, t)
    for m in range(KH):
        tile("FF1", 1, m)
    for t in range(TPH):
        tile("FF2", 1, t)
    return alloc, filled


def block_kernel(nc: bass.Bass, x, w_xdb, w_c, w_z, fc1, fc2, w_out, q_fc, q_proj, cols, rows, out):
    f32, f32r = mybir.dt.float32, mybir.dt.float32r
    ALU = mybir.AluOpType
    ACT = mybir.ActivationFunctionType
    AX = mybir.AxisListType

    alloc, filled = psum_plan()
    BANK = {n: i % RING for i, n in enumerate(alloc)}
    USE = {n: i // RING for i, n in enumerate(alloc)}
    DONE = {n: i + 1 for i, n in enumerate(filled)}

    f_uses = []
    for h in range(2):
        if h == 0:
            f_uses += [("T", 0, 0), ("T", 0, 1)]
        f_uses += [("FC1", h, m) for m in range(KF)]
        if h == 0:
            f_uses += [("T", 1, 0), ("T", 1, 1)]
    f_uses += [("FF1", h, m) for h in range(2) for m in range(KH)]
    FUSE = {n: i for i, n in enumerate(f_uses)}
    hi_uses = []
    for h in range(2):
        hi_uses += [("BT", h)] + [("C", h, i) for i in range(PAIRS)] + [("CUMT", h)]
        if h == 1:
            hi_uses += [("X1T", 0, 0), ("X1T", 0, 1)]
        hi_uses += [("YT", s, t) for s in (2 * h, 2 * h + 1) for t in range(2)]
    hi_uses += [("X1T", 1, 0), ("X1T", 1, 1)]
    HI = {n: i + 1 for i, n in enumerate(hi_uses)}

    with ExitStack() as ctx:
        def sb(name, shape, dt=f32):
            return ctx.enter_context(nc.sbuf_tensor(name, shape, dt))

        def sem(name):
            return ctx.enter_context(nc.semaphore(name))

        with nc.sbuf_tensor("q_raw", [P, 2, KD * H2], f32) as q_raw:
            pass
        decay = sb("decay", [P, ESLOTS, 2, BLK])
        with nc.sbuf_tensor("xn", [P, TPH, D], f32) as xn, nc.sbuf_tensor("q_below", [P, KD * H2], f32) as q_below:
            pass
        yt_hi, yt_lo = sb("yt_hi", [P, KI, SL], f32r), sb("yt_lo", [P, KI, SL], f32r)
        sb("q_below_end", [P, KD * H2 + TPH * D - 2 * KI * SL])

        xs = sb("xs", [P, NT, D])
        feat_hi = sb("feat_hi", [P, KD, HALF], f32r)
        feat_lo = sb("feat_lo", [P, KD, HALF], f32r)
        ftmp = sb("ftmp", [P, FSLOTS, HALF])
        stage = sb("stage", [P, 3, F1])
        wx_hi, wx_lo = sb("wx_hi", [P, KD, WX], f32r), sb("wx_lo", [P, KD, WX], f32r)
        wc_hi, wc_lo = sb("wc_hi", [P, KD, DI], f32r), sb("wc_lo", [P, KD, DI], f32r)
        wz_hi, wz_lo = sb("wz_hi", [P, KD, DI], f32r), sb("wz_lo", [P, KD, DI], f32r)
        f1_hi, f1_lo = sb("f1_hi", [P, KD, F1], f32r), sb("f1_lo", [P, KD, F1], f32r)
        f2_hi, f2_lo = sb("f2_hi", [P, KF, D], f32r), sb("f2_lo", [P, KF, D], f32r)
        wo_hi, wo_lo = sb("wo_hi", [P, KI, D], f32r), sb("wo_lo", [P, KI, D], f32r)
        q1, q2 = sb("q1", [P, KD, H2], f32r), sb("q2", [P, KH, D], f32r)
        bt_hi, bt_lo = sb("bt_hi", [P, HALF], f32r), sb("bt_lo", [P, HALF], f32r)
        ct_hi, ct_lo = sb("ct_hi", [P, PAIRS, HALF], f32r), sb("ct_lo", [P, PAIRS, HALF], f32r)
        zs = sb("zs", [P, TPH, DI])
        xd = sb("xd", [P, TPH, XD])
        xdt = sb("xdt", [P, 2, DI])
        yb = sb("yb", [P, 2, DI])
        g_hi, g_lo = sb("g_hi", [P, KF, HALF], f32r), sb("g_lo", [P, KF, HALF], f32r)
        colv = sb("colv", [P, 2 * KD + KF + KI])
        rowv = sb("rowv", [P, 3 * NH + D])
        ident = sb("ident", [P, P])
        tri1 = sb("tri1", [P, 2, P])
        sel_f = sb("sel_f", [40, NH])
        sel = sb("sel", [40, NH, P], f32r)
        cumt = sb("cumt", [40, HALF], f32r)
        cums = sb("cums", [P, TPH, NH])
        dtw = sb("dtw", [P, 8, TPH, NH])
        expa = sb("expa", [P, NH])
        st = sb("st", [P, NT, 6])
        mv = sb("mv", [P, NT, 2])
        vare = sb("vare", [P, 3 * SEQS, 2])
        mhalf = sb("mhalf", [P, 2])
        rstd = sb("rstd", [P, NT])
        ssq = sb("ssq", [P, NT])
        mse = sb("mse", [P, SEQS, 2])
        rsy = sb("rsy", [P, NT])
        absum = sb("absum", [P, 2])
        am = sb("am", [P, 2])
        thr = sb("thr", [P, 2, 2])
        am11 = sb("am11", [P, 1])
        qscale = sb("qscale", [P, 1])

        LNW, LNB, FB1, NW = 0, KD, 2 * KD, 2 * KD + KF
        banks = [ctx.enter_context(nc.psum_tensor(f"bank{i}", [P, 512], f32)) for i in range(RING)]
        ybank = [ctx.enter_context(nc.psum_tensor(f"ybank{i}", [P, DI], f32)) for i in range(2)]

        x_in = [sem(f"x_in{s}") for s in range(SEQS)]
        w_in = [sem(f"w_in{u}") for u in range(8)]
        q_in = sem("q_in")
        vec_in = sem("vec_in")
        stored = sem("stored")
        zeroed = sem("zeroed")
        consts = sem("consts")
        sel_ready = sem("sel_ready")
        w_hi = sem("w_hi")
        w_lo = sem("w_lo")
        w_lo_pool = sem("w_lo_pool")
        absum_ready = sem("absum_ready")
        q_ready = sem("q_ready")
        var_ready = sem("var_ready")
        eps_added = sem("eps_added")
        rstd_ready = sem("rstd_ready")
        xn_ready = sem("xn_ready")
        x1_ready = sem("x1_ready")
        psum_filled = sem("psum_filled")
        bank_read = [sem(f"bank_read{i}") for i in range(RING)]
        hi_taken = sem("hi_taken")
        f_split = sem("f_split")
        h_ready = sem("h_ready")
        relu_done = sem("relu_done")
        expa_ready = sem("expa_ready")
        u_abs = sem("u_abs")
        u_exp = sem("u_exp")
        dt_ready = sem("dt_ready")
        cums_ready = sem("cums_ready")
        masked = sem("masked")
        xdt_ready = sem("xdt_ready")
        dx_ready = sem("dx_ready")
        y_summed = sem("y_summed")
        y_read = sem("y_read")
        yg_ready = sem("yg_ready")
        ssq_ready = sem("ssq_ready")
        mse_ready = sem("mse_ready")
        rsy_ready = sem("rsy_ready")
        out_ready = sem("out_ready")
        dve_step = sem("dve_step")

        block = ctx.enter_context(nc.Block())

        def wait_filled(eng, *name):
            eng.wait_ge(psum_filled, DONE[name])

        def wait_read(eng, *name):
            eng.wait_ge(bank_read[BANK[name]], USE[name] + 1)

        def bank(*name):
            return banks[BANK[name]]

        def done_with(*name):
            return bank_read[BANK[name]]

        x_t = x.rearrange("(t p) d -> p t d", p=P)
        out_t = out.rearrange("(t p) d -> p t d", p=P)
        pieces = [
            (w_xdb.rearrange("(k p) n -> p k n", p=P), KD, WX),
            (w_c.rearrange("(k p) n -> p k n", p=P), KD, DI),
            (w_z.rearrange("(k p) n -> p k n", p=P), KD, DI),
            (fc1[0:P, :].rearrange("(k p) n -> p k n", p=P), 1, F1),
            (fc1[P:D, :].rearrange("(k p) n -> p k n", p=P), 1, F1),
            (fc2[0:F1 // 2, :].rearrange("(k p) n -> p k n", p=P), KF // 2, D),
            (fc2[F1 // 2:F1, :].rearrange("(k p) n -> p k n", p=P), KF // 2, D),
            (w_out.rearrange("(k p) n -> p k n", p=P), KI, D),
        ]
        piece_hi = [wx_hi[:], wc_hi[:], wz_hi[:], f1_hi[:, 0:1, :], f1_hi[:, 1:2, :],
                    f2_hi[:, 0:KF // 2, :], f2_hi[:, KF // 2:KF, :], wo_hi[:]]
        piece_lo = [wx_lo[:], wc_lo[:], wz_lo[:], f1_lo[:, 0:1, :], f1_lo[:, 1:2, :],
                    f2_lo[:, 0:KF // 2, :], f2_lo[:, KF // 2:KF, :], wo_lo[:]]

        def staged(u):
            _, k, n = pieces[u]
            return stage[:, u % 3, 0:k * n].rearrange("p (k n) -> p k n", k=k)

        @block.sync
        def _(sp):
            def load_x(s):
                sp.dma_start(xs[:, 2 * s:2 * s + 2, :], x_t[:, 2 * s:2 * s + 2, :]).then_inc(x_in[s], 16)

            def load_w(u):
                sp.dma_start(staged(u), pieces[u][0]).then_inc(w_in[u], 16)

            load_x(0)
            load_w(0)
            load_x(1)
            load_w(1)
            load_w(2)
            sp.wait_ge(w_lo, 1)
            load_w(3)
            sp.wait_ge(w_lo, 2)
            load_w(4)
            load_x(2)
            load_x(3)
            sp.dma_start(q_raw[:, 0, :].rearrange("p (k n) -> p k n", k=KD),
                         q_fc.rearrange("(k p) n -> p k n", p=P)).then_inc(q_in, 16)
            sp.dma_start(q_raw[:, 1, :].rearrange("p (k n) -> p k n", k=KH),
                         q_proj.rearrange("(k p) n -> p k n", p=P)).then_inc(q_in, 16)
            sp.wait_ge(w_lo, 3)
            load_w(5)
            sp.wait_ge(w_lo_pool, 1)
            load_w(6)
            sp.wait_ge(w_lo_pool, 2)
            load_w(7)
            for t in range(NT):
                sp.wait_ge(out_ready, t + 1)
                sp.dma_start(out_t[:, t, :], xs[:, t, :]).then_inc(stored, 16)
            sp.wait_ge(stored, 16 * NT)

        @block.tensor
        def _(pe):
            def take(*name):
                if USE[name] > 0:
                    pe.wait_ge(bank_read[BANK[name]], USE[name])
                return banks[BANK[name]]

            def split_product(dst, lhs, rhs, n):
                steps = [(a, c, k) for k in range(n) for a, c in ((0, 0), (0, 1), (1, 0))]
                for i, (a, c, k) in enumerate(steps):
                    last = nc.tensor.matmul(dst, lhs(k)[a], rhs(k)[c], start=i == 0, stop=i == len(steps) - 1)
                return last

            def transposes(name, src, tiles):
                dst = take(*name)
                for j in range(2):
                    for k in range(KD):
                        last = nc.tensor.transpose(dst[:, k * SL + j * P:k * SL + (j + 1) * P],
                                                   src[:, tiles + j, k * P:(k + 1) * P], ident[:])
                last.then_inc(psum_filled, 1)

            def feat(k, c0=0, n=HALF):
                return feat_hi[:, k, c0:c0 + n], feat_lo[:, k, c0:c0 + n]

            def in_projection(h):
                for b in range(2):
                    pe.wait_ge(f_split, FUSE[("T", h, b)] + 1)
                    if h == 0 and b == 0:
                        pe.wait_ge(w_hi, 1)
                        pe.wait_ge(w_lo, 1)
                    dst = take("XD", h, b)
                    for j in range(2):
                        last = split_product(dst[:, j * XD:(j + 1) * XD],
                                             lambda k, c=(2 * b + j) * P: feat(k, c, P),
                                             lambda k: (wx_hi[:, k, 0:XD], wx_lo[:, k, 0:XD]), KD)
                    last.then_inc(psum_filled, 1)
                dst = take("BT", h)
                split_product(dst[:], lambda k: (wx_hi[:, k, XD:WX], wx_lo[:, k, XD:WX]), feat,
                              KD).then_inc(psum_filled, 1)
                if h == 0:
                    pe.wait_ge(w_hi, 2)
                    pe.wait_ge(w_lo, 2)
                for i in range(PAIRS):
                    dst = take("C", h, i)
                    split_product(dst[:], lambda k, c=i * P: (wc_hi[:, k, c:c + P], wc_lo[:, k, c:c + P]), feat,
                                  KD).then_inc(psum_filled, 1)
                if h == 0:
                    pe.wait_ge(w_hi, 3)
                    pe.wait_ge(w_lo, 3)
                for t in range(TPH):
                    dst = take("Z", h, t)
                    split_product(dst[:], lambda k, c=t * P: feat(k, c, P),
                                  lambda k: (wz_hi[:, k, :], wz_lo[:, k, :]), KD).then_inc(psum_filled, 1)

            def mlp_up(h):
                if h == 0:
                    pe.wait_ge(w_hi, 5)
                    pe.wait_ge(w_lo_pool, 2)
                for m in range(KF):
                    dst = take("FC1", h, m)
                    split_product(dst[:], lambda k, c=m * P: (f1_hi[:, k, c:c + P], f1_lo[:, k, c:c + P]), feat,
                                  KD).then_inc(psum_filled, 1)

            def running_sums(h):
                pe.wait_ge(dt_ready, h + 1)
                tri, one = tri1[:, 0, :], tri1[:, 1, :]
                da = dtw[:, 7, :, :]
                dst = take("CUMS", h)
                for b in range(2):
                    c = 2 * b * NH
                    nc.tensor.matmul(dst[:, c:c + NH], tri, da[:, 2 * b, :], start=True, stop=True)
                    nc.tensor.matmul(dst[:, c + NH:c + 2 * NH], one, da[:, 2 * b, :], start=True, stop=False)
                    last = nc.tensor.matmul(dst[:, c + NH:c + 2 * NH], tri, da[:, 2 * b + 1, :],
                                            start=False, stop=True)
                last.then_inc(psum_filled, 1)
                dst = take("CUMT", h)
                for b in range(2):
                    c = b * SL
                    nc.tensor.matmul(dst[0:NH, c:c + SL], da[:, 2 * b, :], tri1[:].rearrange("p a c -> p (a c)"),
                                     start=True, stop=False)
                    last = nc.tensor.matmul(dst[0:NH, c + P:c + SL], da[:, 2 * b + 1, :], tri,
                                            start=False, stop=True)
                last.then_inc(psum_filled, 1)

            def scores(s, i):
                c0 = (s % 2) * SL
                dst = take("CB", s, i)
                for a in range(2):
                    last = nc.tensor.matmul(dst[:, a * SL:(a + 1) * SL], sel[:, a * REP + i, :],
                                            cumt[:, c0:c0 + SL], start=True, stop=True)
                last.then_inc(psum_filled, 1)
                dsts = [take("G", s, i, 0), take("G", s, i, 1)]
                for key in range(2):
                    keys = slice(c0 + key * P, c0 + (key + 1) * P)
                    queries = slice(c0 + key * P, c0 + SL)
                    place = slice(0, SL) if key == 0 else slice(SL, BLK)
                    for n, (u, v) in enumerate(((bt_hi, ct_hi), (bt_hi, ct_lo), (bt_lo, ct_hi))):
                        for a in range(2):
                            rows_a = slice(a * HD, (a + 1) * HD)
                            last = nc.tensor.matmul(dsts[a][:, place], u[rows_a, keys], v[rows_a, i, queries],
                                                    start=n == 0, stop=n == 2)
                            if key == 1 and n == 2:
                                last.then_inc(psum_filled, 1)

            def scan_outputs(s, i):
                n = s * PAIRS + i
                wait_read(pe, "G", s, i, 1)
                if i == 0:
                    pe.wait_ge(xdt_ready, s + 1)
                    if s > 0:
                        pe.wait_ge(ssq_ready, 2 * s)
                for a in range(2):
                    e = decay[:, n % ESLOTS, a, :]
                    hc = slice((a * REP + i) * HD, (a * REP + i + 1) * HD)
                    nc.tensor.matmul(ybank[0][:, hc], e[:, 0:P], xdt[:, 0, hc], start=True, stop=True)
                    nc.tensor.matmul(ybank[1][:, hc], e[:, P:SL], xdt[:, 0, hc], start=True, stop=False)
                    last = nc.tensor.matmul(ybank[1][:, hc], e[:, SL:BLK], xdt[:, 1, hc], start=False, stop=True)
                last.then_inc(y_summed, 1)

            def mlp_down(s, j):
                if s == 0 and j == 0:
                    pe.wait_ge(w_hi, 7)
                    pe.wait_ge(w_lo_pool, 4)
                if j == 0 and s % 2 == 0:
                    pe.wait_ge(f_split, FUSE[("FC1", s // 2, KF - 1)] + 1)
                c = ((s % 2) * 2 + j) * P
                split_product(take("FW", s, j)[:, 0:D],
                              lambda k: (g_hi[:, k, c:c + P], g_lo[:, k, c:c + P]),
                              lambda k: (f2_hi[:, k, :], f2_lo[:, k, :]), KF)

            def y_transposes(s, j):
                pe.wait_ge(yg_ready, 2 * s + j + 1)
                dst = take("YT", s, j)
                for k in range(KI):
                    last = nc.tensor.transpose(dst[:, k * P:(k + 1) * P], yb[:, j, k * P:(k + 1) * P], ident[:])
                last.then_inc(psum_filled, 1)

            def out_projection(s, j):
                if s == 0 and j == 0:
                    pe.wait_ge(w_hi, 8)
                    pe.wait_ge(w_lo, 4)
                wait_read(pe, "YT", s, j)
                split_product(bank("FW", s, j)[:, D:2 * D],
                              lambda k: (yt_hi[:, k, j * P:(j + 1) * P], yt_lo[:, k, j * P:(j + 1) * P]),
                              lambda k: (wo_hi[:, k, :], wo_lo[:, k, :]), KI).then_inc(psum_filled, 1)

            def mixer(s):
                lag = 2
                for i in range(PAIRS):
                    scores(s, i)
                    if i >= lag:
                        scan_outputs(s, i - lag)
                mlp_down(s, 0)
                for i in range(PAIRS - lag, PAIRS):
                    scan_outputs(s, i)
                mlp_down(s, 1)
                for j in range(2):
                    y_transposes(s, j)
                for j in range(2):
                    out_projection(s, j)

            def ternary_up(h):
                for m in range(KH):
                    dst = take("FF1", h, m)
                    for n in range(2 * KD):
                        k = n // 2
                        last = nc.tensor.matmul(dst[:], q1[:, k, m * P:(m + 1) * P], feat(k)[n % 2],
                                                start=n == 0, stop=n == 2 * KD - 1)
                    last.then_inc(psum_filled, 1)

            def ternary_down(h):
                pe.wait_ge(f_split, FUSE[("FF1", h, KH - 1)] + 1)
                for t in range(TPH):
                    dst = take("FF2", h, t)
                    for n in range(2 * KH):
                        k = n // 2
                        last = nc.tensor.matmul(dst[:, 0:D], (g_hi, g_lo)[n % 2][:, k, t * P:(t + 1) * P], q2[:, k, :],
                                                start=n == 0, stop=n == 2 * KH - 1)
                    last.then_inc(psum_filled, 1)

            pe.wait_ge(consts, 1)
            for b in range(2):
                pe.wait_ge(xn_ready, b + 1)
                transposes(("T", 0, b), xn, 2 * b)
            in_projection(0)
            mlp_up(0)
            pe.wait_ge(absum_ready, 2)
            nc.tensor.matmul(take("AM")[:, 0:2], tri1[:, 1, :], absum[:], start=True, stop=True).then_inc(psum_filled, 1)
            running_sums(0)
            for b in range(2):
                pe.wait_ge(xn_ready, 3 + b)
                transposes(("T", 1, b), xn, 2 * b)
            wait_read(pe, "CUMT", 0)
            pe.wait_ge(sel_ready, 1)
            mixer(0)
            mixer(1)
            in_projection(1)
            mlp_up(1)
            running_sums(1)
            for b in range(2):
                pe.wait_ge(x1_ready, b + 1)
                transposes(("X1T", 0, b), xs, 2 * b)
            wait_read(pe, "CUMT", 1)
            mixer(2)
            mixer(3)
            wait_read(pe, "X1T", 0, 1)
            pe.wait_ge(q_ready, 2)
            ternary_up(0)
            for b in range(2):
                pe.wait_ge(x1_ready, 3 + b)
                transposes(("X1T", 1, b), xs, TPH + 2 * b)
            ternary_down(0)
            wait_read(pe, "X1T", 1, 1)
            ternary_up(1)
            ternary_down(1)

        @block.scalar
        def _(act):
            def weight_hi(u):
                act.wait_ge(w_in[u], 16)
                if u == 7:
                    for k in range(KI):
                        last = nc.scalar.activation(piece_hi[u][:, k, :], staged(u)[:, k, :], ACT.Copy,
                                                    scale=colv[:, NW + k:NW + k + 1])
                else:
                    last = nc.scalar.activation(piece_hi[u], staged(u), ACT.Copy)
                last.then_inc(w_hi, 1)

            def f_slot(*name):
                n = FUSE[name]
                if n >= FSLOTS:
                    act.wait_ge(f_split, n - FSLOTS + 1)
                return ftmp[:, n % FSLOTS, :]

            def features(h, b):
                wait_filled(act, "T", h, b)
                f = f_slot("T", h, b)
                src = bank("T", h, b)
                for k in range(KD):
                    last = nc.scalar.activation(f[:, k * SL:(k + 1) * SL], src[:, k * SL:(k + 1) * SL], ACT.Identity,
                                                scale=colv[:, LNW + k:LNW + k + 1], bias=colv[:, LNB + k:LNB + k + 1])
                last.then_inc(done_with("T", h, b), 1)

            def hi_part(name, dst, src):
                wait_filled(act, *name)
                nc.scalar.activation(dst, src, ACT.Copy).then_inc(hi_taken, 1)

            def projections(h):
                for b in range(2):
                    wait_filled(act, "XD", h, b)
                    nc.scalar.activation(xd[:, 2 * b:2 * b + 2, :],
                                         bank("XD", h, b)[:, 0:2 * XD].rearrange("p (t n) -> p t n", t=2),
                                         ACT.Copy).then_inc(done_with("XD", h, b), 1)
                if h == 0:
                    weight_hi(2)
                hi_part(("BT", h), bt_hi[:], bank("BT", h)[:])
                for i in range(PAIRS):
                    hi_part(("C", h, i), ct_hi[:, i, :], bank("C", h, i)[:])
                act.wait_ge(u_abs, h + 1)
                nc.scalar.activation(dtw[:, 2, :, :], dtw[:, 1, :, :], ACT.Exp, scale=-1.0).then_inc(u_exp, 1)
                if h == 0:
                    weight_hi(3)
                    weight_hi(4)
                for t in range(TPH):
                    wait_filled(act, "Z", h, t)
                    nc.scalar.activation(zs[:, t, :], bank("Z", h, t)[:], ACT.Silu).then_inc(done_with("Z", h, t), 1)

            def gelus(h):
                for m in range(KF):
                    wait_filled(act, "FC1", h, m)
                    nc.scalar.activation(f_slot("FC1", h, m), bank("FC1", h, m)[:], ACT.Gelu_apprx_tanh,
                                         bias=colv[:, FB1 + m:FB1 + m + 1]).then_inc(done_with("FC1", h, m), 1)

            def sums_out(h):
                wait_filled(act, "CUMS", h)
                nc.scalar.activation(cums[:], bank("CUMS", h)[:, 0:TPH * NH].rearrange("p (t n) -> p t n", t=TPH),
                                     ACT.Copy).then_inc(done_with("CUMS", h), 1)
                hi_part(("CUMT", h), cumt[0:NH, :], bank("CUMT", h)[0:NH, :])

            def decays(s, i):
                n = s * PAIRS + i
                t0 = (s % 2) * 2
                if s % 2 == 0 and i == 0:
                    wait_read(act, "CUMS", s // 2)
                if n >= ESLOTS:
                    act.wait_ge(y_summed, n - ESLOTS + 1)
                wait_filled(act, "CB", s, i)
                src = bank("CB", s, i)
                for a in range(2):
                    head = a * REP + i
                    e = decay[:, n % ESLOTS, a, :]
                    nc.scalar.activation(e[:, 0:SL], src[:, a * SL:(a + 1) * SL], ACT.Exp, scale=-1.0,
                                         bias=cums[:, t0, head:head + 1])
                    last = nc.scalar.activation(e[:, SL:BLK], src[:, a * SL + P:(a + 1) * SL], ACT.Exp, scale=-1.0,
                                                bias=cums[:, t0 + 1, head:head + 1])
                last.then_inc(done_with("CB", s, i), 1)

            def mixer_out(s):
                for j in range(2):
                    act.wait_ge(yg_ready, 2 * s + j + 1)
                    nc.scalar.activation(ybank[j][:], yb[:, j, :], ACT.Square,
                                         accum_out=ssq[:, 2 * s + j:2 * s + j + 1]).then_inc(ssq_ready, 1)
                for j in range(2):
                    hi_part(("YT", s, j), yt_hi[:, :, j * P:(j + 1) * P],
                            bank("YT", s, j)[:].rearrange("p (k t) -> p k t", k=KI))

            def x1_features(h, b):
                hi_part(("X1T", h, b), feat_hi[:, :, b * SL:(b + 1) * SL],
                        bank("X1T", h, b)[:].rearrange("p (k t) -> p k t", k=KD))

            def squared_relus(h):
                for m in range(KH):
                    wait_filled(act, "FF1", h, m)
                    f = f_slot("FF1", h, m)
                    nc.scalar.activation(f, bank("FF1", h, m)[:], ACT.Relu).then_inc(done_with("FF1", h, m), 1)
                    wait_read(act, "FF1", h, m)
                    nc.scalar.activation(f, f, ACT.Square).then_inc(h_ready, 1)

            act.dma_start(colv[:], cols).then_inc(vec_in, 16)
            act.dma_start(rowv[:], rows.broadcast_to([P, 3 * NH + D])).then_inc(vec_in, 16)
            weight_hi(0)
            act.wait_ge(vec_in, 32)
            nc.scalar.activation(expa[:], rowv[:, NH:2 * NH], ACT.Exp).then_inc(expa_ready, 1)
            features(0, 0)
            weight_hi(1)
            features(0, 1)
            projections(0)
            weight_hi(5)
            gelus(0)
            sums_out(0)
            features(1, 0)
            features(1, 1)
            weight_hi(6)
            weight_hi(7)
            for s in (0, 1):
                for i in range(PAIRS):
                    decays(s, i)
                mixer_out(s)
            projections(1)
            gelus(1)
            sums_out(1)
            x1_features(0, 0)
            x1_features(0, 1)
            for s in (2, 3):
                for i in range(PAIRS):
                    decays(s, i)
                mixer_out(s)
            squared_relus(0)
            x1_features(1, 0)
            x1_features(1, 1)
            squared_relus(1)

        @block.vector
        def _(dve):
            steps = [0]

            def mark(ins):
                ins.then_inc(dve_step, 1)
                steps[0] += 1
                return steps[0]

            def link(ins):
                dve.wait_ge(dve_step, mark(ins))

            def statistics(tiles, signal):
                for j, t in enumerate(tiles):
                    link(nc.vector.bn_stats(st[:, t, :], xs[:, t, :]))
                    last = nc.vector.bn_aggr(mv[:, t, :], st[:, t, :])
                    if j < len(tiles) - 1:
                        mark(last)
                last.then_inc(signal, 1)

            def normalise(t, dst):
                return nc.vector.tensor_scalar(dst, xs[:, t, :], mv[:, t, 0:1], rstd[:, t:t + 1],
                                               ALU.subtract, ALU.mult)

            def first_norm_statistics(s):
                dve.wait_ge(x_in[s], 16)
                statistics((2 * s, 2 * s + 1), var_ready)

            def first_norm(s):
                dve.wait_ge(rstd_ready, s + 1)
                if s >= 2:
                    wait_filled(dve, "T", 0, s - 2)
                for j in range(2):
                    last = normalise(2 * s + j, xn[:, 2 * (s % 2) + j, :])
                last.then_inc(xn_ready, 1)

            def doubled_residual(s):
                dve.wait_ge(xn_ready, s + 1)
                for j in range(2):
                    last = nc.vector.scalar_tensor_tensor(xs[:, 2 * s + j, :], xs[:, 2 * s + j, :], 2.0,
                                                          rowv[:, 3 * NH:], ALU.mult, ALU.add)
                return mark(last)

            def weight_lo(u):
                dve.wait_ge(w_hi, u + 1)
                if u == 7:
                    for k in range(KI):
                        last = nc.vector.scalar_tensor_tensor(piece_lo[u][:, k, :], staged(u)[:, k, :],
                                                              colv[:, NW + k:NW + k + 1],
                                                              piece_hi[u][:, k, :].bitcast(f32), ALU.mult,
                                                              ALU.subtract)
                else:
                    last = nc.vector.tensor_tensor(piece_lo[u], staged(u), piece_hi[u].bitcast(f32), ALU.subtract)
                last.then_inc(w_lo, 1)

            def split_f(name, hi, lo, view):
                f = view(ftmp[:, FUSE[name] % FSLOTS, :])
                n = mark(nc.vector.tensor_copy(hi, f))
                dve.wait_ge(dve_step, n)
                nc.vector.tensor_tensor(lo, f, hi.bitcast(f32), ALU.subtract).then_inc(f_split, 1)

            def features(h, b):
                wait_read(dve, "T", h, b)
                cols_b = slice(b * SL, (b + 1) * SL)
                split_f(("T", h, b), feat_hi[:, :, cols_b], feat_lo[:, :, cols_b],
                        lambda f: f.rearrange("p (k t) -> p k t", k=KD))

            def lo_part(name, dst, src, hi):
                dve.wait_ge(hi_taken, HI[name])
                nc.vector.tensor_tensor(dst, src, hi.bitcast(f32), ALU.subtract).then_inc(done_with(*name), 1)

            def step_inputs(h):
                for b in range(2):
                    wait_read(dve, "XD", h, b)
                link(nc.vector.tensor_tensor(dtw[:, 0, :, :], xd[:, :, XD - NH:XD],
                                             rowv[:, 0:NH].unsqueeze(1).broadcast_to([P, TPH, NH]), ALU.add))
                nc.vector.scalar_tensor_tensor(dtw[:, 1, :, :], dtw[:, 0, :, :], -1.0, dtw[:, 0, :, :], ALU.mult,
                                               ALU.max).then_inc(u_abs, 1)

            def step_sizes(h):
                dve.wait_ge(u_exp, h + 1)
                u, e, r, s, s2, q, dt, da = (dtw[:, n, :, :] for n in (0, 2, 3, 4, 5, 3, 6, 7))
                link(nc.vector.tensor_scalar(r, e, 2.0, None, ALU.add))
                link(nc.vector.reciprocal(s2, r))
                link(nc.vector.tensor_tensor(s, e, s2, ALU.mult))
                link(nc.vector.tensor_tensor(s2, s, s, ALU.mult))
                link(nc.vector.tensor_scalar(q, s2, 1.0 / 17, None, ALU.mult))
                for n in (15, 13, 11, 9, 7, 5, 3):
                    link(nc.vector.scalar_tensor_tensor(q, q, 1.0 / n, s2, ALU.add, ALU.mult))
                link(nc.vector.scalar_tensor_tensor(q, q, 1.0, s, ALU.add, ALU.mult))
                link(nc.vector.tensor_scalar(s, u, 0.0, None, ALU.max))
                link(nc.vector.scalar_tensor_tensor(dt, q, 2.0, s, ALU.mult, ALU.add))
                if h == 0:
                    dve.wait_ge(expa_ready, 1)
                nc.vector.tensor_tensor(da, dt, expa[:].unsqueeze(1).broadcast_to([P, TPH, NH]), ALU.mult)\
                    .then_inc(dt_ready, 1)

            def projections(h):
                if h == 0:
                    weight_lo(2)
                step_inputs(h)
                lo_part(("BT", h), bt_lo[:], bank("BT", h)[:], bt_hi[:])
                for i in range(PAIRS):
                    lo_part(("C", h, i), ct_lo[:, i, :], bank("C", h, i)[:], ct_hi[:, i, :])
                step_sizes(h)

            def ternary_sums():
                dve.wait_ge(q_in, 32)
                for n in range(2):
                    nc.vector.tensor_reduce(absum[:, n:n + 1], q_raw[:, n, :], AX.X, ALU.add,
                                            apply_absolute_value=True).then_inc(absum_ready, 1)

            def ternary_weights():
                wait_filled(dve, "AM")
                link(nc.vector.tensor_scalar(am[:], bank("AM")[:, 0:2], 1.0 / (D * H2), 1e-5, ALU.mult, ALU.max))
                nc.vector.tensor_tensor(am11[:], am[:, 0:1], am[:, 0:1], ALU.mult).then_inc(done_with("AM"), 1)
                mark(nc.vector.tensor_scalar(thr[:, 0, :], am[:], 0.7, None, ALU.mult))
                link(nc.vector.tensor_scalar(thr[:, 1, :], am[:], -0.7, None, ALU.mult))
                mark(nc.vector.tensor_tensor(qscale[:], am11[:], am[:, 1:2], ALU.mult))
                for n, q in enumerate((q1, q2)):
                    flat = q[:].rearrange("p k n -> p (k n)")
                    below = q_below[:]
                    if n > 0:
                        dve.wait_ge(q_ready, n)
                    link(nc.vector.tensor_scalar(below, q_raw[:, n, :], thr[:, 1, n:n + 1], None, ALU.is_lt))
                    nc.vector.scalar_tensor_tensor(flat, q_raw[:, n, :], thr[:, 0, n:n + 1], below,
                                                   ALU.is_gt, ALU.subtract).then_inc(q_ready, 1)

            def gelu_parts(h):
                for m in range(KF):
                    wait_read(dve, "FC1", h, m)
                    split_f(("FC1", h, m), g_hi[:, m, :], g_lo[:, m, :], lambda f: f)

            def sums_out(h):
                lo_part(("CUMT", h), cumt[32:32 + NH, :], bank("CUMT", h)[0:NH, :], cumt[0:NH, :])

            def weighted_scores(s, i):
                n = s * PAIRS + i
                dve.wait_ge(masked, n + 1)
                for a in range(2):
                    wait_filled(dve, "G", s, i, a)
                    e = decay[:, n % ESLOTS, a, :]
                    nc.vector.tensor_tensor(e, bank("G", s, i, a)[:, 0:BLK], e, ALU.mult)\
                        .then_inc(done_with("G", s, i, a), 1)

            def gated(s):
                dve.wait_ge(y_summed, (s + 1) * PAIRS)
                dve.wait_ge(dx_ready, s + 1)
                for j in range(2):
                    nc.vector.tensor_tensor(yb[:, j, :], ybank[j][:], yb[:, j, :], ALU.add).then_inc(y_read, 1)
                for j in range(2):
                    t = (s % 2) * 2 + j
                    wait_read(dve, "Z", s // 2, t)
                    dve.wait_ge(y_read, 2 * s + j + 1)
                    nc.vector.tensor_tensor(yb[:, j, :], yb[:, j, :], zs[:, t, :], ALU.mult).then_inc(yg_ready, 1)
                for j in range(2):
                    lo_part(("YT", s, j), yt_lo[:, :, j * P:(j + 1) * P],
                            bank("YT", s, j)[:].rearrange("p (k t) -> p k t", k=KI), yt_hi[:, :, j * P:(j + 1) * P])

            def joined(s):
                dve.wait_ge(rsy_ready, s + 1)
                marks = []
                for j in range(2):
                    t = 2 * s + j
                    wait_filled(dve, "FW", s, j)
                    marks.append(mark(nc.vector.scalar_tensor_tensor(xs[:, t, :], bank("FW", s, j)[:, D:2 * D],
                                                                     rsy[:, t:t + 1], xs[:, t, :], ALU.mult,
                                                                     ALU.add)))
                for j in range(2):
                    t = 2 * s + j
                    dve.wait_ge(dve_step, marks[j])
                    nc.vector.tensor_tensor(xs[:, t, :], bank("FW", s, j)[:, 0:D], xs[:, t, :], ALU.add)\
                        .then_inc(done_with("FW", s, j), 1)

            def second_norm(s):
                for j in range(2):
                    wait_read(dve, "FW", s, j)
                statistics((2 * s, 2 * s + 1), var_ready)
                dve.wait_ge(rstd_ready, SEQS + s + 1)
                for j in range(2):
                    last = normalise(2 * s + j, xs[:, 2 * s + j, :])
                last.then_inc(x1_ready, 1)

            def x1_features(h, b):
                cols_b = slice(b * SL, (b + 1) * SL)
                lo_part(("X1T", h, b), feat_lo[:, :, cols_b],
                        bank("X1T", h, b)[:].rearrange("p (k t) -> p k t", k=KD), feat_hi[:, :, cols_b])

            def squared_parts(h):
                for m in range(KH):
                    dve.wait_ge(h_ready, h * KH + m + 1)
                    split_f(("FF1", h, m), g_hi[:, m, :], g_lo[:, m, :], lambda f: f)

            def outputs(h, pair):
                tiles = [h * TPH + 2 * pair + j for j in range(2)]
                for j, t in enumerate(tiles):
                    wait_filled(dve, "FF2", h, 2 * pair + j)
                    if j == 0:
                        dve.wait_ge(x1_ready, t // 2 + 1)
                    nc.vector.scalar_tensor_tensor(xs[:, t, :], bank("FF2", h, 2 * pair + j)[:, 0:D], qscale[:],
                                                   xs[:, t, :], ALU.mult, ALU.add)\
                        .then_inc(done_with("FF2", h, 2 * pair + j), 1)
                for j, t in enumerate(tiles):
                    wait_read(dve, "FF2", h, 2 * pair + j)
                statistics(tiles, var_ready)
                dve.wait_ge(rstd_ready, 2 * SEQS + tiles[0] // 2 + 1)
                for t in tiles:
                    normalise(t, xs[:, t, :]).then_inc(out_ready, 1)

            first_norm_statistics(0)
            weight_lo(0)
            first_norm(0)
            first_norm_statistics(1)
            dve.wait_ge(vec_in, 32)
            first_norm(1)
            features(0, 0)
            weight_lo(1)
            features(0, 1)
            dve.wait_ge(consts, 1)
            nc.vector.tensor_copy(sel[:], sel_f[:].unsqueeze(2).broadcast_to([40, NH, P])).then_inc(sel_ready, 1)
            projections(0)
            first_norm_statistics(2)
            first_norm_statistics(3)
            first_norm(2)
            first_norm(3)
            ternary_sums()
            gelu_parts(0)
            ternary_weights()
            weight_lo(7)
            for s in range(SEQS):
                last = doubled_residual(s)
            sums_out(0)
            features(1, 0)
            features(1, 1)
            dve.wait_ge(dve_step, last)
            for s in (0, 1):
                for i in range(PAIRS):
                    weighted_scores(s, i)
                    if i == 1 and s == 1:
                        second_norm(0)
                gated(s)
                joined(s)
            projections(1)
            second_norm(1)
            gelu_parts(1)
            sums_out(1)
            x1_features(0, 0)
            x1_features(0, 1)
            for s in (2, 3):
                for i in range(PAIRS):
                    weighted_scores(s, i)
                    if i == 1 and s == 3:
                        second_norm(2)
                gated(s)
                joined(s)
            second_norm(3)
            squared_parts(0)
            x1_features(1, 0)
            x1_features(1, 1)
            outputs(0, 0)
            outputs(0, 1)
            squared_parts(1)
            outputs(1, 0)
            outputs(1, 1)

        @block.gpsimd
        def _(pool):
            def rstd_of(n, tiles):
                pool.wait_ge(var_ready, n)
                k = len(tiles)
                nc.gpsimd.tensor_scalar(vare[:, n - 1, 0:k], mv[:, tiles[0]:tiles[0] + k, 1], EPS, None, ALU.add)\
                    .then_inc(eps_added, 1)
                pool.wait_ge(eps_added, n)
                nc.gpsimd.tensor_tensor(rstd[:, tiles[0]:tiles[0] + k], vare[:, n - 1, 0:k], mhalf[:, 0:k], ALU.pow)\
                    .then_inc(rstd_ready, 1)

            def weight_lo(u):
                pool.wait_ge(w_hi, u + 1)
                nc.gpsimd.tensor_tensor(piece_lo[u], staged(u), piece_hi[u].bitcast(f32), ALU.subtract)\
                    .then_inc(w_lo_pool, 1)

            def by_head(v):
                return v.rearrange("p (g r d) -> p g r d", g=GROUPS, r=REP)

            def x_heads(s, j):
                t = (s % 2) * 2 + j
                return xd[:, t, 0:GROUPS * HD].rearrange("p (g d) -> p g d", g=GROUPS)\
                    .unsqueeze(2).broadcast_to([P, GROUPS, REP, HD])

            def per_head(v):
                return v.rearrange("p (g r) -> p g r", g=GROUPS).unsqueeze(3).broadcast_to([P, GROUPS, REP, HD])

            def stepped_x(s):
                if s % 2 == 0:
                    pool.wait_ge(dt_ready, s // 2 + 1)
                if s > 0:
                    pool.wait_ge(y_summed, s * PAIRS)
                for j in range(2):
                    t = (s % 2) * 2 + j
                    last = nc.gpsimd.tensor_tensor(by_head(xdt[:, j, :]), x_heads(s, j), per_head(dtw[:, 6, t, :]),
                                                   ALU.mult)
                last.then_inc(xdt_ready, 1)

            def skipped_x(s):
                if s > 0:
                    wait_filled(pool, "YT", s - 1, 1)
                    pool.wait_ge(ssq_ready, 2 * s)
                for j in range(2):
                    last = nc.gpsimd.tensor_tensor(by_head(yb[:, j, :]), x_heads(s, j),
                                                   per_head(rowv[:, 2 * NH:3 * NH]), ALU.mult)
                last.then_inc(dx_ready, 1)

            def mask(s, i):
                n = s * PAIRS + i
                wait_read(pool, "CB", s, i)
                for a in range(2):
                    e = decay[:, n % ESLOTS, a, :].rearrange("p (k t) -> p k t", t=P)[:, 0:3:2, :]
                    last = nc.gpsimd.affine_select(out=e, in_=e, compare_op=ALU.is_ge, fill=0.0, base=0,
                                                   pattern=[[0, 2], [1, P]], channel_multiplier=-1)
                last.then_inc(masked, 1)

            def mixer_scale(s):
                pool.wait_ge(ssq_ready, 2 * s + 2)
                nc.gpsimd.tensor_scalar(mse[:, s, :], ssq[:, 2 * s:2 * s + 2], 1.0 / DI, EPS, ALU.mult, ALU.add)\
                    .then_inc(mse_ready, 1)
                pool.wait_ge(mse_ready, s + 1)
                nc.gpsimd.tensor_tensor(rsy[:, 2 * s:2 * s + 2], mse[:, s, :], mhalf[:], ALU.pow).then_inc(rsy_ready, 1)

            def mixer(s):
                mask(s, 0)
                stepped_x(s)
                for i in range(1, PAIRS):
                    mask(s, i)
                skipped_x(s)
                mixer_scale(s)

            nc.gpsimd.memset(mhalf[:], -0.5)
            nc.gpsimd.memset(ident[:], 0.0).then_inc(zeroed, 1)
            nc.gpsimd.memset(tri1[:], 1.0).then_inc(zeroed, 1)
            nc.gpsimd.memset(sel_f[:], 0.0).then_inc(zeroed, 1)
            nc.gpsimd.memset(cumt[:].bitcast(f32), 0.0).then_inc(zeroed, 1)
            pool.wait_ge(zeroed, 4)
            nc.gpsimd.affine_select(out=ident[:], in_=ident[:], compare_op=ALU.not_equal, fill=1.0, base=0,
                                    pattern=[[-1, P]], channel_multiplier=1)
            nc.gpsimd.affine_select(out=tri1[:, 0, :], in_=tri1[:, 0, :], compare_op=ALU.is_ge, fill=0.0, base=0,
                                    pattern=[[1, P]], channel_multiplier=-1)
            nc.gpsimd.affine_select(out=sel_f[:], in_=sel_f[:], compare_op=ALU.not_equal, fill=1.0, base=0,
                                    pattern=[[-1, NH]], channel_multiplier=1).then_inc(zeroed, 1)
            pool.wait_ge(zeroed, 5)
            nc.gpsimd.affine_select(out=sel_f[:], in_=sel_f[:], compare_op=ALU.not_equal, fill=1.0, base=-32,
                                    pattern=[[-1, NH]], channel_multiplier=1).then_inc(consts, 1)
            rstd_of(1, (0, 1))
            rstd_of(2, (2, 3))
            weight_lo(3)
            weight_lo(4)
            rstd_of(3, (4, 5))
            rstd_of(4, (6, 7))
            weight_lo(5)
            weight_lo(6)
            mixer(0)
            mask(1, 0)
            stepped_x(1)
            mask(1, 1)
            rstd_of(5, (0, 1))
            mask(1, 2)
            mask(1, 3)
            skipped_x(1)
            mixer_scale(1)
            rstd_of(6, (2, 3))
            mixer(2)
            mask(3, 0)
            stepped_x(3)
            mask(3, 1)
            rstd_of(7, (4, 5))
            mask(3, 2)
            mask(3, 3)
            skipped_x(3)
            mixer_scale(3)
            rstd_of(8, (6, 7))
            for n in range(SEQS):
                rstd_of(9 + n, (2 * n, 2 * n + 1))


def kernel(**inputs):
    import numpy as np
    import concourse.bacc as bacc
    from concourse.bass_utils import run_bass_kernel_spmd

    a = {n.removeprefix("L0_"): np.asarray(v) for n, v in inputs.items()}
    w = a["attn_W_in"]
    xb0, b0, c0, dt0 = DI, DI + P, DI + 2 * P, 2 * DI + 2 * P
    w_c = w[:, c0:c0 + DI].reshape(D, GROUPS, REP, HD).transpose(0, 2, 1, 3).reshape(D, DI)
    arrays = {
        "x": a["attn_hidden_states"].reshape(T, D),
        "w_xdb": np.concatenate([w[:, xb0:xb0 + P], w[:, dt0:dt0 + NH], w[:, b0:b0 + P]], axis=1),
        "w_c": w_c,
        "w_z": w[:, 0:DI],
        "fc1": a["attn_fc1_w"],
        "fc2": a["attn_fc2_w"],
        "w_out": a["attn_W_out"],
        "q_fc": a["ffn_w_fc"].T,
        "q_proj": a["ffn_w_proj"].T,
        "cols": np.concatenate([a[n].reshape(-1, P).T for n in ("attn_ln_w", "attn_ln_b", "attn_fc1_b", "attn_norm_w")],
                               axis=1),
        "rows": np.concatenate([a[n] for n in ("attn_dt_bias", "attn_A_log", "attn_D", "attn_fc2_b")])[None, :],
    }
    arrays = {n: np.ascontiguousarray(v) for n, v in arrays.items()}
    nc = bacc.Bacc("TRN2", target_bir_lowering=False, num_devices=1)
    args = [nc.dram_tensor(n, v.shape, mybir.dt.from_np(v.dtype), kind="ExternalInput").ap() for n, v in arrays.items()]
    out = nc.dram_tensor("out", (T, D), mybir.dt.float32, kind="ExternalOutput").ap()
    block_kernel(nc, *args, out)
    result = run_bass_kernel_spmd(nc, [arrays], core_ids=[0])
    return result.results[0]["out"].reshape(SEQS, SL, D)
```

```python
import concourse.bass as bass
from concourse import mybir
from contextlib import ExitStack

P = 128
D = 256
KD = D // P
T = 1024
NT = T // P
SEQS = 4
SL = T // SEQS
HALF = T // 2
TPH = HALF // P
NH = 8
HD = 64
GROUPS = 2
REP = NH // GROUPS
DI = NH * HD
KI = DI // P
F1 = 1024
KF = F1 // P
H2 = 640
KH = H2 // P
HP = (KH + 1) // 2
XD = GROUPS * HD + NH
WX = XD + GROUPS * HD
EPS = 1e-5
RING = 6
FSLOTS = 3
PAIRS = REP
ESLOTS = 4
BLK = SL + P


def tensor_order():
    def pair(s, i):
        return [("G", s, i, 0), ("G", s, i, 1)]

    def sums_of_decays(s):
        return [("CB", s, i) for i in range(PAIRS)]

    def ternary_up(s):
        return [("FF1", s, m) for m in range(HP)]

    def ternary_down(s):
        return [("FF2", s, 0), ("FF2", s, 1)]

    order = [("T", 0, 0), ("T", 0, 1), ("XD", 0, 0), ("XD", 0, 1), ("XT", 0), ("AM",), ("BT", 0), ("C", 0, 0)]
    for h in range(2):
        s0, s1 = 2 * h, 2 * h + 1
        order += [("XT", 1)] * h + [("C", h, i) for i in range(1, PAIRS)] + [("Z", h, i) for i in range(PAIRS)]
        order += [("FC1", h, m) for m in range(4)] + [("CUMS", h), ("CUMT", h), ("FC1", h, 4), ("FC1", h, 5)]
        sums = sums_of_decays(s0)
        order += sums[0:2] + pair(s0, 0) + [("FC1", h, 6), sums[2]] + pair(s0, 1) + [sums[3], ("SCAN", s0, 0)]
        order += [("FC1", h, 7)]
        order += pair(s0, 2) + [("SCAN", s0, 1)] + pair(s0, 3) + [("SCAN", s0, 2)]
        order += sums_of_decays(s1) + [("SCAN", s0, 3)] + pair(s1, 0) + [("DOWN", s0, 0)] + pair(s1, 1)
        order += [("DOWN", s0, 1), ("SCAN", s1, 0), ("OUT", s0, 0), ("SS", s0), ("OUT", s0, 1)]
        if h == 0:
            order += [("T", 1, 0), ("T", 1, 1)] + pair(s1, 2) + [("SCAN", s1, 1)] + pair(s1, 3)
            order += [("SCAN", s1, 2), ("DOWN", s1, 0), ("SCAN", s1, 3), ("XD", 1, 0), ("DOWN", s1, 1), ("XD", 1, 1)]
            order += [("OUT", s1, 0), ("OUT", s1, 1), ("SS", s1), ("BT", 1), ("C", 1, 0)]
        else:
            order += pair(s1, 2) + [("X1T", 0), ("SCAN", s1, 1)] + pair(s1, 3) + [("DOWN", s1, 0), ("SCAN", s1, 2)]
            order += ternary_up(0) + [("SCAN", s1, 3), ("X1T", 1)] + [("DOWN", s1, 1)] + ternary_down(0)
            order += [("OUT", s1, 0), ("OUT", s1, 1), ("SS", s1)] + ternary_up(1) + [("X1T", 2), ("FF2", 1, 0)]
    order += ternary_up(2) + [("FF2", 1, 1), ("X1T", 3), ("FF2", 2, 0)] + ternary_up(3) + [("FF2", 2, 1)]
    order += ternary_down(3)
    return order


def psum_plan():
    alloc, filled = [], []
    for step in tensor_order():
        kind = step[0]
        if kind in ("DOWN", "OUT"):
            if step[2] == 0:
                alloc.append(step[:2])
            else:
                filled.append(step[:2])
        elif kind != "SCAN":
            alloc.append(step)
            filled.append(step)
    return alloc, filled


def block_kernel(nc: bass.Bass, x, w_xdb, w_c, w_z, fc1, fc2, w_out, q_fc, q_proj, cols, rows, b2, out):
    f32, f32r = mybir.dt.float32, mybir.dt.float32r
    ALU = mybir.AluOpType
    ACT = mybir.ActivationFunctionType
    AX = mybir.AxisListType

    alloc, filled = psum_plan()
    BANK = {n: i % RING for i, n in enumerate(alloc)}
    USE = {n: i // RING for i, n in enumerate(alloc)}
    DONE = {n: i + 1 for i, n in enumerate(filled)}

    f_uses = [("T", 0, 0), ("T", 0, 1)] + [("FC1", 0, m) for m in range(KF)] + [("T", 1, 0), ("T", 1, 1)]
    f_uses += [("FC1", 1, m) for m in range(KF)] + [("FF1", s, m) for s in range(SEQS) for m in range(HP)]
    FUSE = {n: i for i, n in enumerate(f_uses)}
    ON_VECTOR = (5, KF - 1)
    F_SPLITS = [n for n in f_uses if n[0] != "FC1" or n[2] in ON_VECTOR]
    GELU_SPLITS = [n[1:] for n in f_uses if n[0] == "FC1" and n[2] not in ON_VECTOR]
    hi_uses = []
    for h in range(2):
        hi_uses += [("BT", h)] + [("C", h, i) for i in range(PAIRS)] + [("CUMT", h)]
    hi_uses += [("X1T", s) for s in range(SEQS)]
    HI = {n: i + 1 for i, n in enumerate(hi_uses)}

    NORMS = [("first", s) for s in range(SEQS)] + [("second", 0), ("second", 1), ("second", 2), ("third", 0),
                                                   ("second", 3), ("third", 1), ("third", 2), ("third", 3)]

    with ExitStack() as ctx:
        def sb(name, shape, dt=f32):
            return ctx.enter_context(nc.sbuf_tensor(name, shape, dt))

        def sem(name):
            return ctx.enter_context(nc.semaphore(name))

        with nc.sbuf_tensor("q_raw", [P, 2, KD * H2], f32) as q_raw:
            pass
        decay = sb("decay", [P, ESLOTS, 2, BLK])
        with nc.sbuf_tensor("q_below", [P, KD * H2], f32) as q_below:
            pass
        yt_hi, yt_lo = sb("yt_hi", [P, KI, SL], f32r), sb("yt_lo", [P, KI, SL], f32r)
        with nc.sbuf_tensor("stage", [P, 3, F1], f32) as stage:
            pass
        sq = sb("sq", [P, PAIRS, SL])
        xdt = sb("xdt", [P, 2, DI])
        yb = sb("yb", [P, PAIRS, SL])
        with (nc.sbuf_tensor("wx_hi", [P, KD, WX], f32r) as wx_hi, nc.sbuf_tensor("wx_lo", [P, KD, WX], f32r) as wx_lo,
              nc.sbuf_tensor("wc_hi", [P, KD, DI], f32r) as wc_hi, nc.sbuf_tensor("wc_lo", [P, KD, DI], f32r) as wc_lo,
              nc.sbuf_tensor("wz_hi", [P, KD, DI], f32r) as wz_hi, nc.sbuf_tensor("wz_lo", [P, KD, DI], f32r) as wz_lo):
            pass
        h_hi, h_lo = sb("h_hi", [P, 2, KH, SL], f32r), sb("h_lo", [P, 2, KH, SL], f32r)
        sb("w_in_end", [P, 2 * KD * (WX + 2 * DI) - 4 * KH * SL])

        xn = sb("xn", [P, 2, 2, D])
        xs = sb("xs", [P, NT, D])
        feat_hi = sb("feat_hi", [P, KD, HALF], f32r)
        feat_lo = sb("feat_lo", [P, KD, HALF], f32r)
        ftmp = sb("ftmp", [P, FSLOTS, HALF])
        f1_hi, f1_lo = sb("f1_hi", [P, KD, F1], f32r), sb("f1_lo", [P, KD, F1], f32r)
        f2_hi, f2_lo = sb("f2_hi", [P, KF, D], f32r), sb("f2_lo", [P, KF, D], f32r)
        wo_hi, wo_lo = sb("wo_hi", [P, KI, D], f32r), sb("wo_lo", [P, KI, D], f32r)
        q1, q2 = sb("q1", [P, KD, H2], f32r), sb("q2", [P, KH, D], f32r)
        b_hh = sb("b_hh", [P, GROUPS, HALF], f32r)
        b_ll = sb("b_ll", [P, GROUPS, HALF], f32r)
        c_hl = sb("c_hl", [P, GROUPS, PAIRS, HALF], f32r)
        with nc.sbuf_tensor("b2_row", [1, D], f32) as b2_row:
            pass
        xt = sb("xt", [P, HALF])
        zs = sb("zs", [P, PAIRS, HALF])
        xd = sb("xd", [P, TPH, XD])
        g_hi, g_lo = sb("g_hi", [P, KF, HALF], f32r), sb("g_lo", [P, KF, HALF], f32r)
        colv = sb("colv", [P, 2 * KD + KF + KI + PAIRS])
        rowv = sb("rowv", [P, 2 * NH])
        b2_hl = sb("b2_hl", [64, D], f32r)
        ident = sb("ident", [P, P])
        tri1 = sb("tri1", [P, 2, P])
        sel_f = sb("sel_f", [40, NH])
        sel = sb("sel", [40, NH, P], f32r)
        cumt = sb("cumt", [40, HALF], f32r)
        cums = sb("cums", [P, TPH, NH])
        dtw = sb("dtw", [P, 8, TPH, NH])
        expa = sb("expa", [P, NH])
        ones_r = sb("ones_r", [64, P], f32r)
        st = sb("st", [P, NT, 6])
        mv = sb("mv", [P, NT, 2])
        vare = sb("vare", [P, 3 * SEQS, 2])
        mhalf = sb("mhalf", [P, 2])
        rstd = sb("rstd", [P, NT])
        mse = sb("mse", [P, SEQS, 2])
        rsy = sb("rsy", [P, NT])
        absum = sb("absum", [P, 2])
        am = sb("am", [P, 2])
        thr = sb("thr", [P, 2, 2])
        am11 = sb("am11", [P, 1])
        qscale = sb("qscale", [P, 1])

        LNW, LNB, FB1, NW, DV = 0, KD, 2 * KD, 2 * KD + KF, 2 * KD + KF + KI
        banks = [ctx.enter_context(nc.psum_tensor(f"bank{i}", [P, 512], f32)) for i in range(RING)]
        ybank = [ctx.enter_context(nc.psum_tensor(f"ybank{i}", [P, DI], f32)) for i in range(2)]

        x_in = [sem(f"x_in{s}") for s in range(SEQS)]
        w_in = [sem(f"w_in{u}") for u in range(8)]
        q_in = sem("q_in")
        vec_in = sem("vec_in")
        b2_in = sem("b2_in")
        stored = sem("stored")
        zeroed = sem("zeroed")
        consts = sem("consts")
        sel_ready = sem("sel_ready")
        w_hi = sem("w_hi")
        w_lo = sem("w_lo")
        w_lo_pool = sem("w_lo_pool")
        absum_ready = sem("absum_ready")
        q_ready = sem("q_ready")
        var_ready = sem("var_ready")
        eps_added = sem("eps_added")
        rstd_ready = sem("rstd_ready")
        xn_ready = sem("xn_ready")
        x1_ready = sem("x1_ready")
        psum_filled = sem("psum_filled")
        bank_read = [sem(f"bank_read{i}") for i in range(RING)]
        hi_taken = sem("hi_taken")
        f_split = sem("f_split")
        h_ready = sem("h_ready")
        relu_done = sem("relu_done")
        expa_ready = sem("expa_ready")
        u_abs = sem("u_abs")
        u_exp = sem("u_exp")
        dt_ready = sem("dt_ready")
        cums_ready = sem("cums_ready")
        masked = sem("masked")
        xdt_ready = sem("xdt_ready")
        y_summed = sem("y_summed")
        y_read = sem("y_read")
        yg_ready = sem("yg_ready")
        yt_copied = sem("yt_copied")
        yt_ready = sem("yt_ready")
        sq_ready = sem("sq_ready")
        sqs_ready = sem("sqs_ready")
        b2_ready = sem("b2_ready")
        g_copied = sem("g_copied")
        g_split = sem("g_split")
        rsy_ready = sem("rsy_ready")
        out_ready = sem("out_ready")
        dve_step = sem("dve_step")

        block = ctx.enter_context(nc.Block())

        def wait_filled(eng, *name):
            eng.wait_ge(psum_filled, DONE[name])

        def wait_split(engine, *name):
            if name[1:] in GELU_SPLITS and name[0] == "FC1":
                engine.wait_ge(g_split, GELU_SPLITS.index(name[1:]) + 1)
            else:
                engine.wait_ge(f_split, F_SPLITS.index(name) + 1)

        def wait_read(eng, *name):
            eng.wait_ge(bank_read[BANK[name]], USE[name] + 1)

        def bank(*name):
            return banks[BANK[name]]

        def done_with(*name):
            return bank_read[BANK[name]]

        x_t = x.rearrange("(t p) d -> p t d", p=P)
        out_t = out.rearrange("(t p) d -> p t d", p=P)
        pieces = [
            (w_xdb.rearrange("(k p) n -> p k n", p=P), KD, WX),
            (w_c.rearrange("(k p) n -> p k n", p=P), KD, DI),
            (w_z.rearrange("(k p) n -> p k n", p=P), KD, DI),
            (fc1[0:P, :].rearrange("(k p) n -> p k n", p=P), 1, F1),
            (fc1[P:D, :].rearrange("(k p) n -> p k n", p=P), 1, F1),
            (fc2[0:F1 // 2, :].rearrange("(k p) n -> p k n", p=P), KF // 2, D),
            (fc2[F1 // 2:F1, :].rearrange("(k p) n -> p k n", p=P), KF // 2, D),
            (w_out.rearrange("(k p) n -> p k n", p=P), KI, D),
        ]
        piece_hi = [wx_hi[:], wc_hi[:], wz_hi[:], f1_hi[:, 0:1, :], f1_hi[:, 1:2, :],
                    f2_hi[:, 0:KF // 2, :], f2_hi[:, KF // 2:KF, :], wo_hi[:]]
        piece_lo = [wx_lo[:], wc_lo[:], wz_lo[:], f1_lo[:, 0:1, :], f1_lo[:, 1:2, :],
                    f2_lo[:, 0:KF // 2, :], f2_lo[:, KF // 2:KF, :], wo_lo[:]]

        def staged(u):
            _, k, n = pieces[u]
            return stage[:, u % 3, 0:k * n].rearrange("p (k n) -> p k n", k=k)

        @block.sync
        def _(sp):
            def load_x(s):
                sp.dma_start(xs[:, 2 * s:2 * s + 2, :], x_t[:, 2 * s:2 * s + 2, :]).then_inc(x_in[s], 16)

            def load_w(u):
                sp.dma_start(staged(u), pieces[u][0]).then_inc(w_in[u], 16)

            load_x(0)
            load_x(1)
            load_w(0)
            load_w(1)
            load_w(2)
            sp.dma_start(q_raw[:, 0, :].rearrange("p (k n) -> p k n", k=KD),
                         q_fc.rearrange("(k p) n -> p k n", p=P)).then_inc(q_in, 16)
            sp.dma_start(q_raw[:, 1, :].rearrange("p (k n) -> p k n", k=KH),
                         q_proj.rearrange("(k p) n -> p k n", p=P)).then_inc(q_in, 16)
            sp.wait_ge(w_lo, 1)
            load_w(3)
            sp.wait_ge(w_lo, 2)
            load_w(4)
            load_x(2)
            load_x(3)
            sp.wait_ge(w_lo, 3)
            load_w(5)
            sp.wait_ge(w_lo_pool, 1)
            load_w(6)
            sp.wait_ge(w_lo_pool, 2)
            load_w(7)
            for t in range(NT):
                sp.wait_ge(out_ready, t + 1)
                sp.dma_start(out_t[:, t, :], xs[:, t, :]).then_inc(stored, 16)
            sp.wait_ge(stored, 16 * NT)

        @block.tensor
        def _(pe):
            def take(*name):
                if USE[name] > 0:
                    pe.wait_ge(bank_read[BANK[name]], USE[name])
                return banks[BANK[name]]

            def product(dst, lhs, rhs, n, start=True):
                steps = [(a, c, k) for k in range(n) for a, c in ((0, 0), (0, 1), (1, 0))]
                for i, (a, c, k) in enumerate(steps):
                    last = nc.tensor.matmul(dst, lhs(k)[a], rhs(k)[c], start=start and i == 0,
                                            stop=i == len(steps) - 1)
                return last

            def feat(k, c0=0, n=HALF):
                return feat_hi[:, k, c0:c0 + n], feat_lo[:, k, c0:c0 + n]

            def transposes(name, src, t0):
                dst = take(*name)
                for j in range(2):
                    for k in range(KD):
                        last = nc.tensor.transpose(dst[:, k * SL + j * P:k * SL + (j + 1) * P],
                                                   src[:, t0 + j, k * P:(k + 1) * P], ident[:])
                last.then_inc(psum_filled, 1)

            def x_transposes(h, b):
                if h == 0 and b == 0:
                    pe.wait_ge(consts, 1)
                pe.wait_ge(xn_ready, 2 * h + b + 1)
                transposes(("T", h, b), xn[:, b, :, :], 0)

            def token_major_x(h, b):
                wait_split(pe, "T", h, b)
                if h == 0 and b == 0:
                    pe.wait_ge(w_hi, 1)
                    pe.wait_ge(w_lo, 1)
                dst = take("XD", h, b)
                for j in range(2):
                    last = product(dst[:, j * XD:(j + 1) * XD], lambda k, c=(2 * b + j) * P: feat(k, c, P),
                                   lambda k: (wx_hi[:, k, 0:XD], wx_lo[:, k, 0:XD]), KD)
                last.then_inc(psum_filled, 1)

            def feature_major(name, hi, lo, c):
                product(take(*name)[:], lambda k: (hi[:, k, c:c + P], lo[:, k, c:c + P]), feat,
                        KD).then_inc(psum_filled, 1)

            def c_features(h, i):
                if h == 0 and i == 0:
                    pe.wait_ge(w_hi, 2)
                    pe.wait_ge(w_lo, 2)
                feature_major(("C", h, i), wc_hi, wc_lo, i * P)

            def z_features(h, i):
                if h == 0 and i == 0:
                    pe.wait_ge(w_hi, 3)
                    pe.wait_ge(w_lo, 3)
                feature_major(("Z", h, i), wz_hi, wz_lo, i * P)

            def mlp_up(h, m):
                if h == 0 and m == 0:
                    pe.wait_ge(w_hi, 5)
                    pe.wait_ge(w_lo_pool, 2)
                feature_major(("FC1", h, m), f1_hi, f1_lo, m * P)

            def weight_means():
                pe.wait_ge(absum_ready, 2)
                nc.tensor.matmul(take("AM")[:, 0:2], tri1[:, 1, :], absum[:], start=True, stop=True)\
                    .then_inc(psum_filled, 1)

            def sums_by_token(h):
                pe.wait_ge(dt_ready, h + 1)
                tri, one, da = tri1[:, 0, :], tri1[:, 1, :], dtw[:, 7, :, :]
                dst = take("CUMS", h)
                for b in range(2):
                    c = 2 * b * NH
                    nc.tensor.matmul(dst[:, c:c + NH], tri, da[:, 2 * b, :], start=True, stop=True)
                    nc.tensor.matmul(dst[:, c + NH:c + 2 * NH], one, da[:, 2 * b, :], start=True, stop=False)
                    last = nc.tensor.matmul(dst[:, c + NH:c + 2 * NH], tri, da[:, 2 * b + 1, :],
                                            start=False, stop=True)
                last.then_inc(psum_filled, 1)

            def sums_by_head(h):
                da = dtw[:, 7, :, :]
                dst = take("CUMT", h)
                for b in range(2):
                    c = b * SL
                    nc.tensor.matmul(dst[0:NH, c:c + SL], da[:, 2 * b, :], tri1[:].rearrange("p a c -> p (a c)"),
                                     start=True, stop=False)
                    last = nc.tensor.matmul(dst[0:NH, c + P:c + SL], da[:, 2 * b + 1, :], tri1[:, 0, :],
                                            start=False, stop=True)
                last.then_inc(psum_filled, 1)

            def decay_sums(s, i):
                if s % 2 == 0 and i == 0:
                    wait_read(pe, "CUMT", s // 2)
                    if s == 0:
                        pe.wait_ge(sel_ready, 1)
                c0 = (s % 2) * SL
                dst = take("CB", s, i)
                for a in range(2):
                    last = nc.tensor.matmul(dst[:, a * SL:(a + 1) * SL], sel[:, a * REP + i, :],
                                            cumt[:, c0:c0 + SL], start=True, stop=True)
                last.then_inc(psum_filled, 1)

            def scores(s, i, a):
                c0 = (s % 2) * SL
                dst = take("G", s, i, a)
                for key in range(2):
                    keys = slice(c0 + key * P, c0 + (key + 1) * P)
                    queries = slice(c0 + key * P, c0 + SL)
                    place = slice(0, SL) if key == 0 else slice(SL, BLK)
                    nc.tensor.matmul(dst[:, place], b_hh[:, a, keys], c_hl[:, a, i, queries], start=True, stop=False)
                    last = nc.tensor.matmul(dst[:, place], b_ll[:, a, keys], c_hl[:, a, i, queries],
                                            start=False, stop=True)
                last.then_inc(psum_filled, 1)

            def scan(s, i):
                n = s * PAIRS + i
                pe.wait_ge(masked, n + 1)
                if i == 0:
                    pe.wait_ge(xdt_ready, s + 1)
                if i % 2 == 0 and s > 0:
                    pe.wait_ge(y_read, 2 * s + i // 2 - 1)
                for a in range(2):
                    e = decay[:, n % ESLOTS, a, :]
                    head = slice((a * REP + i) * HD, (a * REP + i + 1) * HD)
                    dst = ybank[i // 2][a * HD:(a + 1) * HD, (i % 2) * SL:(i % 2 + 1) * SL]
                    nc.tensor.matmul(dst, xdt[:, 0, head], e[:, 0:SL], start=True, stop=False)
                    last = nc.tensor.matmul(dst[:, P:SL], xdt[:, 1, head], e[:, SL:BLK], start=False, stop=True)
                last.then_inc(y_summed, 1)

            def mlp_down(s, j):
                if s == 0 and j == 0:
                    pe.wait_ge(w_hi, 7)
                    pe.wait_ge(w_lo_pool, 4)
                    pe.wait_ge(b2_ready, 3)
                if j == 0 and s % 2 == 0:
                    for m in (KF - 2, KF - 1):
                        wait_split(pe, "FC1", s // 2, m)
                c = ((s % 2) * 2 + j) * P
                dst = (take("DOWN", s) if j == 0 else bank("DOWN", s))[:, j * D:(j + 1) * D]
                nc.tensor.matmul(dst, ones_r[:], b2_hl[:], start=True, stop=False)
                last = product(dst, lambda k: (g_hi[:, k, c:c + P], g_lo[:, k, c:c + P]),
                               lambda k: (f2_hi[:, k, :], f2_lo[:, k, :]), KF, start=False)
                if j == 1:
                    last.then_inc(psum_filled, 1)

            def out_projection(s, j):
                if s == 0 and j == 0:
                    pe.wait_ge(w_hi, 8)
                    pe.wait_ge(w_lo, 4)
                if j == 0:
                    pe.wait_ge(yt_ready, 2 * s + 2)
                dst = take("OUT", s) if j == 0 else bank("OUT", s)
                last = product(dst[:, j * D:(j + 1) * D],
                               lambda k: (yt_hi[:, k, j * P:(j + 1) * P], yt_lo[:, k, j * P:(j + 1) * P]),
                               lambda k: (wo_hi[:, k, :], wo_lo[:, k, :]), KI)
                if j == 1:
                    last.then_inc(psum_filled, 1)

            def square_sums(s):
                pe.wait_ge(sqs_ready, 2 * s + 2)
                dst = take("SS", s)
                for j in range(2):
                    for k in range(2):
                        last = nc.tensor.matmul(dst[:, 2 * j:2 * j + 2], sq[:, 2 * k, j * P:(j + 1) * P], tri1[:, 1, 0:2],
                                                start=k == 0, stop=k == 1)
                last.then_inc(psum_filled, 1)

            def x1_transposes(s):
                pe.wait_ge(x1_ready, s + 1)
                transposes(("X1T", s), xs, 2 * s)

            def ternary_up(s, m2):
                if m2 == 0:
                    wait_read(pe, "X1T", s)
                    if s == 0:
                        pe.wait_ge(q_ready, 2)
                dst = take("FF1", s, m2)
                c = (s % 2) * SL
                for m in range(2 * m2, min(2 * m2 + 2, KH)):
                    for n in range(2 * KD):
                        last = nc.tensor.matmul(dst[:, (m % 2) * SL:(m % 2 + 1) * SL], q1[:, n // 2, m * P:(m + 1) * P],
                                                feat(n // 2, c, SL)[n % 2], start=n == 0, stop=n == 2 * KD - 1)
                last.then_inc(psum_filled, 1)

            def ternary_down(s, j):
                dst = take("FF2", s, j)
                for m in range(KH):
                    if j == 0 and m % 2 == 0:
                        wait_split(pe, "FF1", s, m // 2)
                    for n, h in enumerate((h_hi, h_lo)):
                        last = nc.tensor.matmul(dst[:, 0:D], h[:, s % 2, m, j * P:(j + 1) * P], q2[:, m, :],
                                                start=m == 0 and n == 0, stop=m == KH - 1 and n == 1)
                last.then_inc(psum_filled, 1)

            stages = {
                "T": x_transposes, "XD": token_major_x, "C": c_features, "Z": z_features, "FC1": mlp_up,
                "XT": lambda h: feature_major(("XT", h), wx_hi, wx_lo, 0),
                "BT": lambda h: feature_major(("BT", h), wx_hi, wx_lo, XD),
                "AM": weight_means, "CUMS": sums_by_token, "CUMT": sums_by_head, "CB": decay_sums,
                "G": scores, "SCAN": scan,
                "DOWN": mlp_down, "OUT": out_projection, "SS": square_sums, "X1T": x1_transposes,
                "FF1": ternary_up, "FF2": ternary_down,
            }
            for step in tensor_order():
                stages[step[0]](*step[1:])

        @block.scalar
        def _(act):
            def weight_hi(u):
                act.wait_ge(w_in[u], 16)
                if u == 7:
                    for k in range(KI):
                        last = nc.scalar.activation(piece_hi[u][:, k, :], staged(u)[:, k, :], ACT.Copy,
                                                    scale=colv[:, NW + k:NW + k + 1])
                else:
                    last = nc.scalar.activation(piece_hi[u], staged(u), ACT.Copy)
                last.then_inc(w_hi, 1)

            def f_slot(*name):
                n = FUSE[name]
                if n >= FSLOTS:
                    wait_split(act, *f_uses[n - FSLOTS])
                return ftmp[:, n % FSLOTS, :]

            def features(h, b):
                wait_filled(act, "T", h, b)
                f = f_slot("T", h, b)
                src = bank("T", h, b)
                for k in range(KD):
                    last = nc.scalar.activation(f[:, k * SL:(k + 1) * SL], src[:, k * SL:(k + 1) * SL], ACT.Identity,
                                                scale=colv[:, LNW + k:LNW + k + 1], bias=colv[:, LNB + k:LNB + k + 1])
                last.then_inc(done_with("T", h, b), 1)

            def token_major_x(h, b):
                wait_filled(act, "XD", h, b)
                nc.scalar.activation(xd[:, 2 * b:2 * b + 2, :],
                                     bank("XD", h, b)[:, 0:2 * XD].rearrange("p (t n) -> p t n", t=2),
                                     ACT.Copy).then_inc(done_with("XD", h, b), 1)

            def x_features(h):
                if h == 0:
                    act.wait_ge(b2_ready, 3)
                wait_filled(act, "XT", h)
                nc.scalar.activation(xt[:], bank("XT", h)[:], ACT.Copy).then_inc(done_with("XT", h), 1)

            def b_features(h):
                wait_filled(act, "BT", h)
                for g in range(GROUPS):
                    for half in range(2):
                        last = nc.scalar.activation(b_hh[half * HD:(half + 1) * HD, g, :],
                                                    bank("BT", h)[g * HD:(g + 1) * HD, :], ACT.Copy)
                last.then_inc(hi_taken, 1)

            def c_features(h, i):
                wait_filled(act, "C", h, i)
                for g in range(GROUPS):
                    last = nc.scalar.activation(c_hl[0:HD, g, i, :], bank("C", h, i)[g * HD:(g + 1) * HD, :], ACT.Copy)
                last.then_inc(hi_taken, 1)

            def step_exponentials(h):
                act.wait_ge(u_abs, h + 1)
                nc.scalar.activation(dtw[:, 2, :, :], dtw[:, 1, :, :], ACT.Exp, scale=-1.0).then_inc(u_exp, 1)

            def gates(h, i):
                wait_filled(act, "Z", h, i)
                nc.scalar.activation(zs[:, i, :], bank("Z", h, i)[:], ACT.Silu).then_inc(done_with("Z", h, i), 1)

            def gelu(h, m):
                wait_filled(act, "FC1", h, m)
                nc.scalar.activation(f_slot("FC1", h, m), bank("FC1", h, m)[:], ACT.Gelu_apprx_tanh,
                                     bias=colv[:, FB1 + m:FB1 + m + 1]).then_inc(done_with("FC1", h, m), 1)

            def sums_out(h):
                wait_filled(act, "CUMS", h)
                nc.scalar.activation(cums[:], bank("CUMS", h)[:, 0:TPH * NH].rearrange("p (t n) -> p t n", t=TPH),
                                     ACT.Copy).then_inc(done_with("CUMS", h), 1)
                wait_filled(act, "CUMT", h)
                nc.scalar.activation(cumt[0:NH, :], bank("CUMT", h)[0:NH, :], ACT.Copy).then_inc(hi_taken, 1)

            def decays(s, i):
                n = s * PAIRS + i
                t0 = (s % 2) * 2
                if n == 0:
                    act.wait_ge(q_ready, 2)
                if s % 2 == 0 and i == 0:
                    wait_read(act, "CUMS", s // 2)
                if n >= ESLOTS:
                    act.wait_ge(y_summed, n - ESLOTS + 1)
                wait_filled(act, "CB", s, i)
                src = bank("CB", s, i)
                for a in range(2):
                    head = a * REP + i
                    e = decay[:, n % ESLOTS, a, :]
                    nc.scalar.activation(e[:, 0:SL], src[:, a * SL:(a + 1) * SL], ACT.Exp, scale=-1.0,
                                         bias=cums[:, t0, head:head + 1])
                    last = nc.scalar.activation(e[:, SL:BLK], src[:, a * SL + P:(a + 1) * SL], ACT.Exp, scale=-1.0,
                                                bias=cums[:, t0 + 1, head:head + 1])
                last.then_inc(done_with("CB", s, i), 1)

            def squares(s, k):
                act.wait_ge(yg_ready, 2 * s + k + 1)
                if s > 0:
                    wait_filled(act, "SS", s - 1)
                nc.scalar.activation(sq[:, 2 * k:2 * k + 2, :], yb[:, 2 * k:2 * k + 2, :], ACT.Square)\
                    .then_inc(sq_ready, 1)

            def mean_squares(s):
                wait_filled(act, "SS", s)
                nc.scalar.activation(mse[:, s, :], bank("SS", s)[:, 0:4:2], ACT.Copy, scale=1.0 / DI, bias=EPS)\
                    .then_inc(done_with("SS", s), 1)

            def x1_features(s):
                wait_filled(act, "X1T", s)
                c = (s % 2) * SL
                nc.scalar.activation(feat_hi[:, :, c:c + SL], bank("X1T", s)[:].rearrange("p (k t) -> p k t", k=KD),
                                     ACT.Copy).then_inc(hi_taken, 1)

            def squared_relus(s):
                for m2 in range(HP):
                    name = ("FF1", s, m2)
                    wait_filled(act, *name)
                    w = SL * min(2, KH - 2 * m2)
                    f = f_slot(*name)[:, 0:w]
                    nc.scalar.activation(f, bank(*name)[:, 0:w], ACT.Relu).then_inc(done_with(*name), 1)
                    wait_read(act, *name)
                    nc.scalar.activation(f, f, ACT.Square).then_inc(h_ready, 1)

            def weight_sums():
                act.wait_ge(q_in, 32)
                for n in range(2):
                    if n > 0:
                        act.wait_ge(absum_ready, n)
                    nc.scalar.activation(q_below[:], q_raw[:, n, :], ACT.Abs, accum_out=absum[:, n:n + 1])\
                        .then_inc(absum_ready, 1)

            act.dma_start(colv[:], cols).then_inc(vec_in, 16)
            act.dma_start(rowv[:], rows.broadcast_to([P, 2 * NH])).then_inc(vec_in, 16)
            act.dma_start(b2_row[:], b2).then_inc(b2_in, 16)
            weight_hi(0)
            act.wait_ge(vec_in, 32)
            nc.scalar.activation(expa[:], rowv[:, NH:2 * NH], ACT.Exp).then_inc(expa_ready, 1)
            features(0, 0)
            weight_hi(1)
            features(0, 1)
            token_major_x(0, 0)
            weight_sums()
            token_major_x(0, 1)
            weight_hi(2)
            weight_hi(3)
            x_features(0)
            weight_hi(4)
            b_features(0)
            c_features(0, 0)
            for h in range(2):
                s0, s1 = 2 * h, 2 * h + 1
                if h == 1:
                    x_features(1)
                for i in range(1, PAIRS):
                    c_features(h, i)
                if h == 0:
                    step_exponentials(0)
                    weight_hi(5)
                for i in range(PAIRS):
                    gates(h, i)
                if h == 0:
                    weight_hi(6)
                gelu(h, 0)
                gelu(h, 1)
                if h == 0:
                    weight_hi(7)
                gelu(h, 2)
                gelu(h, 3)
                sums_out(h)
                gelu(h, 4)
                gelu(h, 5)
                for i in range(PAIRS):
                    decays(s0, i)
                gelu(h, 6)
                gelu(h, 7)
                for i in range(PAIRS):
                    decays(s1, i)
                    if i == 1:
                        squares(s0, 0)
                    if i == 2:
                        squares(s0, 1)
                mean_squares(s0)
                if h == 0:
                    features(1, 0)
                    features(1, 1)
                    squares(1, 0)
                    token_major_x(1, 0)
                    token_major_x(1, 1)
                    squares(1, 1)
                    step_exponentials(1)
                    mean_squares(1)
                    b_features(1)
                    c_features(1, 0)
                else:
                    x1_features(0)
                    squares(3, 0)
                    squared_relus(0)
                    x1_features(1)
                    squares(3, 1)
                    mean_squares(3)
                    squared_relus(1)
                    x1_features(2)
                    squared_relus(2)
            x1_features(3)
            squared_relus(3)

        @block.vector
        def _(dve):
            steps = [0]

            def mark(ins):
                ins.then_inc(dve_step, 1)
                steps[0] += 1
                return steps[0]

            def link(ins):
                dve.wait_ge(dve_step, mark(ins))

            def statistics(tiles):
                marks = [mark(nc.vector.bn_stats(st[:, t, :], xs[:, t, :])) for t in tiles]
                for t, m in zip(tiles, marks):
                    dve.wait_ge(dve_step, m)
                    last = nc.vector.bn_aggr(mv[:, t, :], st[:, t, :])
                last.then_inc(var_ready, 1)

            def normalise(t, dst):
                return nc.vector.tensor_scalar(dst, xs[:, t, :], mv[:, t, 0:1], rstd[:, t:t + 1],
                                               ALU.subtract, ALU.mult)

            def first_norm_statistics(s):
                dve.wait_ge(x_in[s], 16)
                statistics((2 * s, 2 * s + 1))

            def first_norm(s):
                dve.wait_ge(rstd_ready, s + 1)
                if s >= 2:
                    wait_filled(dve, "T", 0, s - 2)
                for j in range(2):
                    last = normalise(2 * s + j, xn[:, s % 2, j, :])
                last.then_inc(xn_ready, 1)

            def weight_lo(u):
                dve.wait_ge(w_hi, u + 1)
                if u == 7:
                    for k in range(KI):
                        last = nc.vector.scalar_tensor_tensor(piece_lo[u][:, k, :], staged(u)[:, k, :],
                                                              colv[:, NW + k:NW + k + 1],
                                                              piece_hi[u][:, k, :].bitcast(f32), ALU.mult,
                                                              ALU.subtract)
                else:
                    last = nc.vector.tensor_tensor(piece_lo[u], staged(u), piece_hi[u].bitcast(f32), ALU.subtract)
                last.then_inc(w_lo, 1)

            def split_f(hi, lo, f):
                link(nc.vector.tensor_copy(hi, f))
                nc.vector.tensor_tensor(lo, f, hi.bitcast(f32), ALU.subtract).then_inc(f_split, 1)

            def f_of(*name):
                return ftmp[:, FUSE[name] % FSLOTS, :]

            def features(h, b):
                wait_read(dve, "T", h, b)
                c = slice(b * SL, (b + 1) * SL)
                split_f(feat_hi[:, :, c], feat_lo[:, :, c],
                        f_of("T", h, b).rearrange("p (k t) -> p k t", k=KD))

            def step_inputs(h):
                for b in range(2):
                    wait_read(dve, "XD", h, b)
                if h == 0:
                    dve.wait_ge(vec_in, 32)
                link(nc.vector.tensor_tensor(dtw[:, 0, :, :], xd[:, :, XD - NH:XD],
                                             rowv[:, 0:NH].unsqueeze(1).broadcast_to([P, TPH, NH]), ALU.add))
                nc.vector.scalar_tensor_tensor(dtw[:, 1, :, :], dtw[:, 0, :, :], -1.0, dtw[:, 0, :, :], ALU.mult,
                                               ALU.max).then_inc(u_abs, 1)

            def step_sizes(h):
                dve.wait_ge(u_exp, h + 1)
                u, e, r, s, s2, q, dt, da = (dtw[:, n, :, :] for n in (0, 2, 3, 4, 5, 3, 6, 7))
                link(nc.vector.tensor_scalar(r, e, 2.0, None, ALU.add))
                link(nc.vector.reciprocal(s2, r))
                link(nc.vector.tensor_tensor(s, e, s2, ALU.mult))
                link(nc.vector.tensor_tensor(s2, s, s, ALU.mult))
                link(nc.vector.tensor_scalar(q, s2, 1.0 / 17, None, ALU.mult))
                for n in (15, 13, 11, 9, 7, 5, 3):
                    link(nc.vector.scalar_tensor_tensor(q, q, 1.0 / n, s2, ALU.add, ALU.mult))
                link(nc.vector.scalar_tensor_tensor(q, q, 1.0, s, ALU.add, ALU.mult))
                link(nc.vector.tensor_scalar(s, u, 0.0, None, ALU.max))
                link(nc.vector.scalar_tensor_tensor(dt, q, 2.0, s, ALU.mult, ALU.add))
                if h == 0:
                    dve.wait_ge(expa_ready, 1)
                nc.vector.tensor_tensor(da, dt, expa[:].unsqueeze(1).broadcast_to([P, TPH, NH]), ALU.mult)\
                    .then_inc(dt_ready, 1)

            def b_features(h):
                dve.wait_ge(hi_taken, HI[("BT", h)])
                for g in range(GROUPS):
                    for half in range(2):
                        r = slice(half * HD, (half + 1) * HD)
                        last = nc.vector.tensor_tensor(b_ll[r, g, :], bank("BT", h)[g * HD:(g + 1) * HD, :],
                                                       b_hh[r, g, :].bitcast(f32), ALU.subtract)
                last.then_inc(done_with("BT", h), 1)

            def c_features(h, i):
                dve.wait_ge(hi_taken, HI[("C", h, i)])
                for g in range(GROUPS):
                    last = nc.vector.tensor_tensor(c_hl[HD:P, g, i, :], bank("C", h, i)[g * HD:(g + 1) * HD, :],
                                                   c_hl[0:HD, g, i, :].bitcast(f32), ALU.subtract)
                last.then_inc(done_with("C", h, i), 1)

            def ternary_means():
                wait_filled(dve, "AM")
                link(nc.vector.tensor_scalar(am[:], bank("AM")[:, 0:2], 1.0 / (D * H2), 1e-5, ALU.mult, ALU.max))
                nc.vector.tensor_tensor(am11[:], am[:, 0:1], am[:, 0:1], ALU.mult).then_inc(done_with("AM"), 1)
                mark(nc.vector.tensor_scalar(thr[:, 0, :], am[:], 0.7, None, ALU.mult))
                link(nc.vector.tensor_scalar(thr[:, 1, :], am[:], -0.7, None, ALU.mult))
                mark(nc.vector.tensor_tensor(qscale[:], am11[:], am[:, 1:2], ALU.mult))

            def ternary_weights(n):
                if n > 0:
                    dve.wait_ge(q_ready, n)
                link(nc.vector.tensor_scalar(q_below[:], q_raw[:, n, :], thr[:, 1, n:n + 1], None, ALU.is_lt))
                nc.vector.scalar_tensor_tensor((q1, q2)[n][:].rearrange("p k n -> p (k n)"), q_raw[:, n, :],
                                               thr[:, 0, n:n + 1], q_below[:], ALU.is_gt, ALU.subtract)\
                    .then_inc(q_ready, 1)

            def gelu_parts(h, m):
                wait_read(dve, "FC1", h, m)
                if m in ON_VECTOR:
                    split_f(g_hi[:, m, :], g_lo[:, m, :], f_of("FC1", h, m))
                else:
                    nc.vector.tensor_copy(g_hi[:, m, :], f_of("FC1", h, m)).then_inc(g_copied, 1)

            def sums_out(h):
                dve.wait_ge(hi_taken, HI[("CUMT", h)])
                nc.vector.tensor_tensor(cumt[32:32 + NH, :], bank("CUMT", h)[0:NH, :], cumt[0:NH, :].bitcast(f32),
                                        ALU.subtract).then_inc(done_with("CUMT", h), 1)

            def weighted_scores(s, i):
                n = s * PAIRS + i
                wait_read(dve, "CB", s, i)
                for a in range(2):
                    wait_filled(dve, "G", s, i, a)
                    e = decay[:, n % ESLOTS, a, :]
                    nc.vector.tensor_tensor(e, bank("G", s, i, a)[:, 0:BLK], e, ALU.mult)\
                        .then_inc(done_with("G", s, i, a), 1)

            def gated(s, k):
                tokens = slice((s % 2) * SL, (s % 2 + 1) * SL)
                pairs = slice(2 * k, 2 * k + 2)
                dve.wait_ge(y_summed, s * PAIRS + 2 * k + 2)
                if s > 0:
                    dve.wait_ge(sq_ready, 2 * s + k - 1)
                for i in (2 * k, 2 * k + 1):
                    last = nc.vector.scalar_tensor_tensor(yb[:, i, :], xt[:, tokens], colv[:, DV + i:DV + i + 1],
                                                          ybank[k][:, (i % 2) * SL:(i % 2 + 1) * SL],
                                                          ALU.mult, ALU.add)
                last.then_inc(y_read, 1)
                dve.wait_ge(y_read, 2 * s + k + 1)
                nc.vector.tensor_tensor(yb[:, pairs, :], yb[:, pairs, :], zs[:, pairs, tokens], ALU.mult)\
                    .then_inc(yg_ready, 1)
                dve.wait_ge(yg_ready, 2 * s + k + 1)
                if s > 0:
                    wait_filled(dve, "OUT", s - 1)
                nc.vector.tensor_copy(yt_hi[:, pairs, :], yb[:, pairs, :]).then_inc(yt_copied, 1)
                dve.wait_ge(yt_copied, 2 * s + k + 1)
                nc.vector.tensor_tensor(yt_lo[:, pairs, :], yb[:, pairs, :], yt_hi[:, pairs, :].bitcast(f32),
                                        ALU.subtract).then_inc(yt_ready, 1)

            def residual(s):
                wait_filled(dve, "DOWN", s)
                x_tiles = xs[:, 2 * s:2 * s + 2, :]
                nc.vector.scalar_tensor_tensor(x_tiles, x_tiles, 2.0,
                                               bank("DOWN", s)[:].rearrange("p (t d) -> p t d", t=2),
                                               ALU.mult, ALU.add).then_inc(done_with("DOWN", s), 1)

            def joined(s):
                dve.wait_ge(rsy_ready, s + 1)
                wait_read(dve, "DOWN", s)
                wait_filled(dve, "OUT", s)
                for j in range(2):
                    t = 2 * s + j
                    last = nc.vector.scalar_tensor_tensor(xs[:, t, :], bank("OUT", s)[:, j * D:(j + 1) * D],
                                                          rsy[:, t:t + 1], xs[:, t, :], ALU.mult, ALU.add)
                last.then_inc(done_with("OUT", s), 1)

            def second_norm_statistics(s):
                wait_read(dve, "OUT", s)
                statistics((2 * s, 2 * s + 1))

            def second_norm(s):
                dve.wait_ge(rstd_ready, NORMS.index(("second", s)) + 1)
                for j in range(2):
                    last = normalise(2 * s + j, xs[:, 2 * s + j, :])
                last.then_inc(x1_ready, 1)

            def x1_features(s):
                dve.wait_ge(hi_taken, HI[("X1T", s)])
                c = (s % 2) * SL
                nc.vector.tensor_tensor(feat_lo[:, :, c:c + SL], bank("X1T", s)[:].rearrange("p (k t) -> p k t", k=KD),
                                        feat_hi[:, :, c:c + SL].bitcast(f32), ALU.subtract)\
                    .then_inc(done_with("X1T", s), 1)

            def squared_parts(s):
                if s >= 2:
                    wait_filled(dve, "FF2", s - 2, 1)
                for m2 in range(HP):
                    dve.wait_ge(h_ready, s * HP + m2 + 1)
                    m = slice(2 * m2, min(2 * m2 + 2, KH))
                    w = SL * (m.stop - m.start)
                    split_f(h_hi[:, s % 2, m, :], h_lo[:, s % 2, m, :],
                            f_of("FF1", s, m2)[:, 0:w].rearrange("p (k t) -> p k t", t=SL))

            def output_sum(s, j):
                t = 2 * s + j
                wait_filled(dve, "FF2", s, j)
                if j == 0:
                    dve.wait_ge(x1_ready, s + 1)
                nc.vector.scalar_tensor_tensor(xs[:, t, :], bank("FF2", s, j)[:, 0:D], qscale[:],
                                               xs[:, t, :], ALU.mult, ALU.add).then_inc(done_with("FF2", s, j), 1)

            def third_norm_statistics(s):
                for j in range(2):
                    wait_read(dve, "FF2", s, j)
                statistics((2 * s, 2 * s + 1))

            def output_sums(s):
                output_sum(s, 0)
                output_sum(s, 1)
                third_norm_statistics(s)

            def outputs(s):
                dve.wait_ge(rstd_ready, NORMS.index(("third", s)) + 1)
                for t in (2 * s, 2 * s + 1):
                    normalise(t, xs[:, t, :]).then_inc(out_ready, 1)

            first_norm_statistics(0)
            first_norm_statistics(1)
            first_norm(0)
            weight_lo(0)
            first_norm(1)
            features(0, 0)
            weight_lo(1)
            features(0, 1)
            dve.wait_ge(consts, 1)
            nc.vector.tensor_copy(sel[:], sel_f[:].unsqueeze(2).broadcast_to([40, NH, P])).then_inc(sel_ready, 1)
            dve.wait_ge(b2_in, 16)
            nc.vector.tensor_copy(ones_r[:], tri1[0:64, 1, :]).then_inc(b2_ready, 1)
            nc.vector.tensor_copy(b2_hl[0:1, :], b2_row[:]).then_inc(b2_ready, 1)
            dve.wait_ge(b2_ready, 2)
            nc.vector.tensor_tensor(b2_hl[32:33, :], b2_row[:], b2_hl[0:1, :].bitcast(f32), ALU.subtract)\
                .then_inc(b2_ready, 1)
            weight_lo(2)
            step_inputs(0)
            ternary_means()
            ternary_weights(0)
            b_features(0)
            c_features(0, 0)
            for h in range(2):
                s0, s1 = 2 * h, 2 * h + 1
                for i in range(1, PAIRS):
                    c_features(h, i)
                if h == 1:
                    second_norm(1)
                step_sizes(h)
                gelu_parts(h, 0)
                gelu_parts(h, 1)
                if h == 0:
                    ternary_weights(1)
                gelu_parts(h, 2)
                if h == 0:
                    weight_lo(7)
                gelu_parts(h, 3)
                sums_out(h)
                gelu_parts(h, 4)
                gelu_parts(h, 5)
                weighted_scores(s0, 0)
                weighted_scores(s0, 1)
                if h == 0:
                    first_norm_statistics(2)
                    first_norm_statistics(3)
                weighted_scores(s0, 2)
                gelu_parts(h, 6)
                weighted_scores(s0, 3)
                gelu_parts(h, 7)
                gated(s0, 0)
                gated(s0, 1)
                weighted_scores(s1, 0)
                weighted_scores(s1, 1)
                if h == 0:
                    first_norm(2)
                    first_norm(3)
                residual(s0)
                joined(s0)
                weighted_scores(s1, 2)
                second_norm_statistics(s0)
                if h == 0:
                    features(1, 0)
                    weighted_scores(1, 3)
                    features(1, 1)
                    second_norm(0)
                    gated(1, 0)
                    gated(1, 1)
                    step_inputs(1)
                    residual(1)
                    joined(1)
                    second_norm_statistics(1)
                    b_features(1)
                    c_features(1, 0)
                else:
                    second_norm(2)
                    x1_features(0)
                    weighted_scores(3, 3)
                    gated(3, 0)
                    squared_parts(0)
                    residual(3)
                    gated(3, 1)
                    x1_features(1)
                    output_sums(0)
            joined(3)
            second_norm_statistics(3)
            squared_parts(1)
            x1_features(2)
            second_norm(3)
            outputs(0)
            output_sum(1, 0)
            squared_parts(2)
            x1_features(3)
            output_sum(1, 1)
            third_norm_statistics(1)
            outputs(1)
            squared_parts(3)
            output_sums(2)
            output_sums(3)
            outputs(2)
            outputs(3)

        @block.gpsimd
        def _(pool):
            def rstd_of(kind, s):
                n = NORMS.index((kind, s))
                pool.wait_ge(var_ready, n + 1)
                nc.gpsimd.tensor_scalar(vare[:, n, :], mv[:, 2 * s:2 * s + 2, 1], EPS, None, ALU.add)\
                    .then_inc(eps_added, 1)
                pool.wait_ge(eps_added, n + 1)
                nc.gpsimd.tensor_tensor(rstd[:, 2 * s:2 * s + 2], vare[:, n, :], mhalf[:], ALU.pow)\
                    .then_inc(rstd_ready, 1)

            def weight_lo(u):
                pool.wait_ge(w_hi, u + 1)
                nc.gpsimd.tensor_tensor(piece_lo[u], staged(u), piece_hi[u].bitcast(f32), ALU.subtract)\
                    .then_inc(w_lo_pool, 1)

            def gelu_lo(h, m):
                pool.wait_ge(g_copied, GELU_SPLITS.index((h, m)) + 1)
                nc.gpsimd.tensor_tensor(g_lo[:, m, :], ftmp[:, FUSE[("FC1", h, m)] % FSLOTS, :],
                                        g_hi[:, m, :].bitcast(f32), ALU.subtract).then_inc(g_split, 1)

            def stepped_x(s):
                if s == 0:
                    pool.wait_ge(w_lo, 4)
                if s % 2 == 0:
                    pool.wait_ge(dt_ready, s // 2 + 1)
                if s > 0:
                    pool.wait_ge(y_summed, s * PAIRS)
                for j in range(2):
                    t = (s % 2) * 2 + j
                    x_heads = xd[:, t, 0:GROUPS * HD].rearrange("p (g d) -> p g d", g=GROUPS)\
                        .unsqueeze(2).broadcast_to([P, GROUPS, REP, HD])
                    dt_heads = dtw[:, 6, t, :].rearrange("p (g r) -> p g r", g=GROUPS)\
                        .unsqueeze(3).broadcast_to([P, GROUPS, REP, HD])
                    last = nc.gpsimd.tensor_tensor(xdt[:, j, :].rearrange("p (g r d) -> p g r d", g=GROUPS, r=REP),
                                                   x_heads, dt_heads, ALU.mult)
                last.then_inc(xdt_ready, 1)

            def mask(s, i):
                n = s * PAIRS + i
                for a in range(2):
                    wait_read(pool, "G", s, i, a)
                    e = decay[:, n % ESLOTS, a, :].rearrange("p (k t) -> p k t", t=P)[:, 0:3:2, :]
                    last = nc.gpsimd.affine_select(out=e, in_=e, compare_op=ALU.is_ge, fill=0.0, base=0,
                                                   pattern=[[0, 2], [1, P]], channel_multiplier=-1)
                last.then_inc(masked, 1)

            def squares(s, k):
                pool.wait_ge(sq_ready, 2 * s + k + 1)
                nc.gpsimd.tensor_tensor(sq[:, 2 * k, :], sq[:, 2 * k, :], sq[:, 2 * k + 1, :], ALU.add)\
                    .then_inc(sqs_ready, 1)

            def mixer_scale(s):
                wait_read(pool, "SS", s)
                nc.gpsimd.tensor_tensor(rsy[:, 2 * s:2 * s + 2], mse[:, s, :], mhalf[:], ALU.pow).then_inc(rsy_ready, 1)

            nc.gpsimd.memset(mhalf[:], -0.5)
            nc.gpsimd.memset(ident[:], 0.0).then_inc(zeroed, 1)
            nc.gpsimd.memset(tri1[:], 1.0).then_inc(zeroed, 1)
            nc.gpsimd.memset(sel_f[:], 0.0).then_inc(zeroed, 1)
            nc.gpsimd.memset(cumt[:].bitcast(f32), 0.0).then_inc(zeroed, 1)
            nc.gpsimd.memset(b2_hl[:].bitcast(f32), 0.0).then_inc(zeroed, 1)
            pool.wait_ge(zeroed, 5)
            nc.gpsimd.affine_select(out=ident[:], in_=ident[:], compare_op=ALU.not_equal, fill=1.0, base=0,
                                    pattern=[[-1, P]], channel_multiplier=1)
            nc.gpsimd.affine_select(out=tri1[:, 0, :], in_=tri1[:, 0, :], compare_op=ALU.is_ge, fill=0.0, base=0,
                                    pattern=[[1, P]], channel_multiplier=-1)
            nc.gpsimd.affine_select(out=sel_f[:], in_=sel_f[:], compare_op=ALU.not_equal, fill=1.0, base=0,
                                    pattern=[[-1, NH]], channel_multiplier=1).then_inc(zeroed, 1)
            pool.wait_ge(zeroed, 6)
            nc.gpsimd.affine_select(out=sel_f[:], in_=sel_f[:], compare_op=ALU.not_equal, fill=1.0, base=-32,
                                    pattern=[[-1, NH]], channel_multiplier=1).then_inc(consts, 1)
            rstd_of("first", 0)
            rstd_of("first", 1)
            for u in (3, 4, 5, 6):
                weight_lo(u)
            for h in range(2):
                s0, s1 = 2 * h, 2 * h + 1
                for m in range(3):
                    gelu_lo(h, m)
                stepped_x(s0)
                gelu_lo(h, 3)
                mask(s0, 0)
                gelu_lo(h, 4)
                mask(s0, 1)
                if h == 0:
                    rstd_of("first", 2)
                    rstd_of("first", 3)
                mask(s0, 2)
                mask(s0, 3)
                gelu_lo(h, 6)
                stepped_x(s1)
                squares(s0, 0)
                squares(s0, 1)
                mask(s1, 0)
                mask(s1, 1)
                mixer_scale(s0)
                mask(s1, 2)
                rstd_of("second", s0)
                mask(s1, 3)
                squares(s1, 0)
                squares(s1, 1)
                if h == 1:
                    rstd_of("third", 0)
                mixer_scale(s1)
                rstd_of("second", s1)
            rstd_of("third", 1)
            rstd_of("third", 2)
            rstd_of("third", 3)


def kernel(**inputs):
    import numpy as np
    import concourse.bacc as bacc
    from concourse.bass_utils import run_bass_kernel_spmd

    a = {n.removeprefix("L0_"): np.asarray(v) for n, v in inputs.items()}
    w = a["attn_W_in"]
    xb0, b0, c0, dt0 = DI, DI + P, DI + 2 * P, 2 * DI + 2 * P

    def paired(m):
        return m.reshape(-1, GROUPS, REP, HD).transpose(0, 2, 1, 3).reshape(-1, DI)

    arrays = {
        "x": a["attn_hidden_states"].reshape(T, D),
        "w_xdb": np.concatenate([w[:, xb0:xb0 + P], w[:, dt0:dt0 + NH], w[:, b0:b0 + P]], axis=1),
        "w_c": paired(w[:, c0:c0 + DI]),
        "w_z": paired(w[:, 0:DI]),
        "fc1": a["attn_fc1_w"],
        "fc2": a["attn_fc2_w"],
        "w_out": paired(a["attn_W_out"].T).T,
        "q_fc": a["ffn_w_fc"].T,
        "q_proj": a["ffn_w_proj"].T,
        "cols": np.concatenate([v.reshape(-1, P).T for v in (
            a["attn_ln_w"], a["attn_ln_b"], a["attn_fc1_b"], paired(a["attn_norm_w"]),
            paired(np.repeat(a["attn_D"], HD)))], axis=1),
        "rows": np.concatenate([a["attn_dt_bias"], a["attn_A_log"]])[None, :],
        "b2": a["attn_fc2_b"][None, :],
    }
    arrays = {n: np.ascontiguousarray(v) for n, v in arrays.items()}
    nc = bacc.Bacc("TRN2", target_bir_lowering=False, num_devices=1)
    args = [nc.dram_tensor(n, v.shape, mybir.dt.from_np(v.dtype), kind="ExternalInput").ap() for n, v in arrays.items()]
    out = nc.dram_tensor("out", (T, D), mybir.dt.float32, kind="ExternalOutput").ap()
    block_kernel(nc, *args, out)
    result = run_bass_kernel_spmd(nc, [arrays], core_ids=[0])
    return result.results[0]["out"].reshape(SEQS, SL, D)
```

```python
import concourse.bass as bass
from concourse import mybir
from contextlib import ExitStack

P = 128
D = 256
KD = D // P
T = 1024
NT = T // P
SEQS = 4
SL = T // SEQS
HALF = T // 2
TPH = HALF // P
NH = 8
HD = 64
GROUPS = 2
REP = NH // GROUPS
DI = NH * HD
KI = DI // P
F1 = 1024
KF = F1 // P
H2 = 640
KH = H2 // P
HP = (KH + 1) // 2
XD = GROUPS * HD + NH
WX = XD + GROUPS * HD
EPS = 1e-5
RING = 6
FSLOTS = 3
PAIRS = REP
ESLOTS = 4
BLK = SL + P


def tensor_order():
    order = [
        ("T", 0, 0), ("T", 0, 1), ("XD", 0, 0), ("XD", 0, 1), ("XT", 0), ("BT", 0), ("AM",), ("C", 0, 0),
    ]
    for h in range(2):
        s0, s1 = 2 * h, 2 * h + 1
        order += [
            ("C", h, 2), ("C", h, 1), ("C", h, 3), ("Z", h, 1), ("Z", h, 2), ("Z", h, 3), ("Z", h, 0),
            ("FC1", h, 0), ("FC1", h, 2), ("FC1", h, 1), ("FC1", h, 3), ("CUMS", h), ("CUMT", h),
            ("FC1", h, 4), ("FC1", h, 5),
        ]
        order += [
            ("CB", s0, 0), ("G", s0, 0, 0), ("CB", s0, 1), ("G", s0, 1, 0), ("G", s0, 0, 1), ("CB", s0, 2),
            ("FC1", h, 6), ("G", s0, 1, 1), ("CB", s0, 3), ("FC1", h, 7), ("G", s0, 2, 1), ("G", s0, 2, 0),
            ("SCAN", s0, 0), ("SCAN", s0, 1), ("G", s0, 3, 0),
        ]
        order += [
            ("CB", s1, 2), ("CB", s1, 0), ("G", s0, 3, 1), ("CB", s1, 1), ("G", s1, 0, 1), ("SCAN", s0, 2),
            ("DOWN", s0, 0), ("SCAN", s0, 3), ("DOWN", s0, 1), ("CB", s1, 3), ("G", s1, 0, 0), ("OUT", s0, 0),
            ("G", s1, 1, 1), ("SS", s0), ("G", s1, 1, 0), ("OUT", s0, 1), ("SCAN", s1, 0),
        ]
        if h == 0:
            order += [
                ("T", 1, 1), ("G", 1, 2, 0), ("G", 1, 2, 1), ("T", 1, 0), ("DOWN", 1, 0), ("G", 1, 3, 0),
                ("G", 1, 3, 1), ("SCAN", 1, 1), ("XD", 1, 0), ("SCAN", 1, 2), ("SCAN", 1, 3), ("DOWN", 1, 1),
                ("XD", 1, 1), ("OUT", 1, 0), ("BT", 1), ("OUT", 1, 1), ("SS", 1), ("XT", 1), ("C", 1, 0),
            ]
    order += [
        ("SCAN", 3, 1), ("G", 3, 2, 1), ("G", 3, 2, 0), ("G", 3, 3, 1), ("G", 3, 3, 0), ("X1T", 0),
        ("DOWN", 3, 0), ("FF1", 0, 0), ("SCAN", 3, 2),
    ]
    order += [
        ("SCAN", 3, 3), ("FF1", 0, 2), ("FF1", 0, 1), ("DOWN", 3, 1), ("X1T", 1), ("OUT", 3, 0), ("X1T", 2),
        ("SS", 3), ("OUT", 3, 1), ("FF2", 0, 0), ("FF1", 1, 0), ("FF2", 0, 1), ("FF1", 1, 1), ("FF1", 2, 1),
        ("FF1", 1, 2), ("X1T", 3), ("FF1", 2, 0), ("FF2", 1, 0), ("FF2", 1, 1), ("FF1", 2, 2), ("FF1", 3, 0),
        ("FF1", 3, 1), ("FF2", 2, 0), ("FF1", 3, 2), ("FF2", 3, 0), ("FF2", 2, 1), ("FF2", 3, 1),
    ]
    return order


def psum_plan():
    alloc, filled = [], []
    for step in tensor_order():
        kind = step[0]
        if kind in ("DOWN", "OUT"):
            if step[2] == 0:
                alloc.append(step[:2])
            else:
                filled.append(step[:2])
        elif kind != "SCAN":
            alloc.append(step)
            filled.append(step)
    return alloc, filled


def block_kernel(nc: bass.Bass, x, w_xdb, w_c, w_z, fc1, fc2, w_out, q_fc, q_proj, cols, rows, b2, out):
    f32, f32r = mybir.dt.float32, mybir.dt.float32r
    ALU = mybir.AluOpType
    ACT = mybir.ActivationFunctionType
    AX = mybir.AxisListType

    alloc, filled = psum_plan()
    BANK = {n: i % RING for i, n in enumerate(alloc)}
    USE = {n: i // RING for i, n in enumerate(alloc)}
    DONE = {n: i + 1 for i, n in enumerate(filled)}

    f_uses = [("T", 0, 0), ("T", 0, 1)] + [("FC1", 0, m) for m in range(KF)] + [("T", 1, 0), ("T", 1, 1)]
    f_uses += [("FC1", 1, m) for m in range(KF)] + [("FF1", s, m) for s in range(SEQS) for m in range(HP)]
    FUSE = {n: i for i, n in enumerate(f_uses)}
    ON_VECTOR = (5, KF - 1)
    F_SPLITS = [n for n in f_uses if n[0] != "FC1" or n[2] in ON_VECTOR]
    GELU_SPLITS = [n[1:] for n in f_uses if n[0] == "FC1" and n[2] not in ON_VECTOR]
    hi_uses = []
    for h in range(2):
        hi_uses += [("BT", h)] + [("C", h, i) for i in range(PAIRS)] + [("CUMT", h)]
    hi_uses += [("X1T", s) for s in range(SEQS)]
    HI = {n: i + 1 for i, n in enumerate(hi_uses)}

    NORMS = [(kind, s) for kind in ("first", "second", "third") for s in range(SEQS)]

    with ExitStack() as ctx:
        def sb(name, shape, dt=f32):
            return ctx.enter_context(nc.sbuf_tensor(name, shape, dt))

        def sem(name):
            return ctx.enter_context(nc.semaphore(name))

        with nc.sbuf_tensor("q_raw", [P, 2, KD * H2], f32) as q_raw:
            pass
        decay = sb("decay", [P, ESLOTS, 2, BLK])
        with nc.sbuf_tensor("q_below", [P, KD * H2], f32) as q_below:
            pass
        yt_hi, yt_lo = sb("yt_hi", [P, KI, SL], f32r), sb("yt_lo", [P, KI, SL], f32r)
        with nc.sbuf_tensor("stage", [P, 3, F1], f32) as stage:
            pass
        sq = sb("sq", [P, PAIRS, SL])
        xdt = sb("xdt", [P, 2, DI])
        yb = sb("yb", [P, PAIRS, SL])
        with (nc.sbuf_tensor("wx_hi", [P, KD, WX], f32r) as wx_hi, nc.sbuf_tensor("wx_lo", [P, KD, WX], f32r) as wx_lo,
              nc.sbuf_tensor("wc_hi", [P, KD, DI], f32r) as wc_hi, nc.sbuf_tensor("wc_lo", [P, KD, DI], f32r) as wc_lo,
              nc.sbuf_tensor("wz_hi", [P, KD, DI], f32r) as wz_hi, nc.sbuf_tensor("wz_lo", [P, KD, DI], f32r) as wz_lo):
            pass
        h_hi, h_lo = sb("h_hi", [P, 2, KH, SL], f32r), sb("h_lo", [P, 2, KH, SL], f32r)
        sb("w_in_end", [P, 2 * KD * (WX + 2 * DI) - 4 * KH * SL])

        xn = sb("xn", [P, 2, 2, D])
        xs = sb("xs", [P, NT, D])
        feat_hi = sb("feat_hi", [P, KD, HALF], f32r)
        feat_lo = sb("feat_lo", [P, KD, HALF], f32r)
        warm = sb("warm", [P, HALF], mybir.dt.bfloat16)
        ftmp = sb("ftmp", [P, FSLOTS, HALF])
        f1_hi, f1_lo = sb("f1_hi", [P, KD, F1], f32r), sb("f1_lo", [P, KD, F1], f32r)
        f2_hi, f2_lo = sb("f2_hi", [P, KF, D], f32r), sb("f2_lo", [P, KF, D], f32r)
        wo_hi, wo_lo = sb("wo_hi", [P, KI, D], f32r), sb("wo_lo", [P, KI, D], f32r)
        q1, q2 = sb("q1", [P, KD, H2], f32r), sb("q2", [P, KH, D], f32r)
        b_hh = sb("b_hh", [P, GROUPS, HALF], f32r)
        b_ll = sb("b_ll", [P, GROUPS, HALF], f32r)
        c_hl = sb("c_hl", [P, GROUPS, PAIRS, HALF], f32r)
        xt = sb("xt", [P, HALF])
        zs = sb("zs", [P, PAIRS, HALF])
        xd = sb("xd", [P, TPH, XD])
        g_hi, g_lo = sb("g_hi", [P, KF, HALF], f32r), sb("g_lo", [P, KF, HALF], f32r)
        colv = sb("colv", [P, 2 * KD + KF + KI + PAIRS])
        rowv = sb("rowv", [P, 2 * NH])
        b2_half = sb("b2_half", [P, D])
        ident = sb("ident", [P, P])
        tri1 = sb("tri1", [P, 2, P])
        sel_f = sb("sel_f", [40, NH])
        sel = sb("sel", [40, NH, P], f32r)
        cumt = sb("cumt", [40, HALF], f32r)
        cums = sb("cums", [P, TPH, NH])
        dtw = sb("dtw", [P, 8, TPH, NH])
        expa = sb("expa", [P, NH])
        st = sb("st", [P, NT, 6])
        mv = sb("mv", [P, NT, 2])
        vare = sb("vare", [P, 3 * SEQS, 2])
        mhalf = sb("mhalf", [P, 2])
        rstd = sb("rstd", [P, NT])
        shift = sb("shift", [P, NT])
        mse = sb("mse", [P, SEQS, 2])
        rsy = sb("rsy", [P, NT])
        absum = sb("absum", [P, 2])
        am = sb("am", [P, 2])
        thr = sb("thr", [P, 2, 2])
        am11 = sb("am11", [P, 1])
        qscale = sb("qscale", [P, 1])

        LNW, LNB, FB1, NW, DV = 0, KD, 2 * KD, 2 * KD + KF, 2 * KD + KF + KI
        banks = [ctx.enter_context(nc.psum_tensor(f"bank{i}", [P, 512], f32)) for i in range(RING)]
        ybank = [ctx.enter_context(nc.psum_tensor(f"ybank{i}", [P, DI], f32)) for i in range(2)]

        x_in = [sem(f"x_in{s}") for s in range(SEQS)]
        w_in = [sem(f"w_in{u}") for u in range(8)]
        q_in = sem("q_in")
        vec_in = sem("vec_in")
        b2_in = sem("b2_in")
        stored = sem("stored")
        warm_ready = sem("warm_ready")
        zeroed = sem("zeroed")
        consts = sem("consts")
        sel_ready = sem("sel_ready")
        w_hi = sem("w_hi")
        w_lo = sem("w_lo")
        w_lo_pool = sem("w_lo_pool")
        absum_ready = sem("absum_ready")
        q_ready = sem("q_ready")
        var_ready = sem("var_ready")
        eps_added = sem("eps_added")
        rstd_ready = sem("rstd_ready")
        xn_ready = sem("xn_ready")
        x1_ready = sem("x1_ready")
        psum_filled = sem("psum_filled")
        bank_read = [sem(f"bank_read{i}") for i in range(RING)]
        hi_taken = sem("hi_taken")
        f_split = sem("f_split")
        h_ready = sem("h_ready")
        expa_ready = sem("expa_ready")
        u_abs = sem("u_abs")
        u_exp = sem("u_exp")
        dt_ready = sem("dt_ready")
        masked = sem("masked")
        xdt_ready = sem("xdt_ready")
        y_summed = sem("y_summed")
        y_read = sem("y_read")
        yg_ready = sem("yg_ready")
        yt_copied = sem("yt_copied")
        yt_ready = sem("yt_ready")
        sq_ready = sem("sq_ready")
        sqs_ready = sem("sqs_ready")
        b2_ready = sem("b2_ready")
        biased = sem("biased")
        g_copied = sem("g_copied")
        g_split = sem("g_split")
        mean_scaled = sem("mean_scaled")
        last_ready = sem("last_ready")
        rsy_ready = sem("rsy_ready")
        out_ready = sem("out_ready")
        dve_step = sem("dve_step")

        block = ctx.enter_context(nc.Block())

        def wait_filled(eng, *name):
            eng.wait_ge(psum_filled, DONE[name])

        def wait_split(engine, *name):
            if name[1:] in GELU_SPLITS and name[0] == "FC1":
                engine.wait_ge(g_split, GELU_SPLITS.index(name[1:]) + 1)
            else:
                engine.wait_ge(f_split, F_SPLITS.index(name) + 1)

        def wait_read(eng, *name):
            eng.wait_ge(bank_read[BANK[name]], USE[name] + 1)

        def bank(*name):
            return banks[BANK[name]]

        def done_with(*name):
            return bank_read[BANK[name]]

        x_t = x.rearrange("(t p) d -> p t d", p=P)
        out_t = out.rearrange("(t p) d -> p t d", p=P)
        pieces = [
            (w_xdb.rearrange("(k p) n -> p k n", p=P), KD, WX),
            (w_c.rearrange("(k p) n -> p k n", p=P), KD, DI),
            (w_z.rearrange("(k p) n -> p k n", p=P), KD, DI),
            (fc1[0:P, :].rearrange("(k p) n -> p k n", p=P), 1, F1),
            (fc1[P:D, :].rearrange("(k p) n -> p k n", p=P), 1, F1),
            (fc2[0:F1 // 2, :].rearrange("(k p) n -> p k n", p=P), KF // 2, D),
            (fc2[F1 // 2:F1, :].rearrange("(k p) n -> p k n", p=P), KF // 2, D),
            (w_out.rearrange("(k p) n -> p k n", p=P), KI, D),
        ]
        piece_hi = [wx_hi[:], wc_hi[:], wz_hi[:], f1_hi[:, 0:1, :], f1_hi[:, 1:2, :],
                    f2_hi[:, 0:KF // 2, :], f2_hi[:, KF // 2:KF, :], wo_hi[:]]
        piece_lo = [wx_lo[:], wc_lo[:], wz_lo[:], f1_lo[:, 0:1, :], f1_lo[:, 1:2, :],
                    f2_lo[:, 0:KF // 2, :], f2_lo[:, KF // 2:KF, :], wo_lo[:]]

        def staged(u):
            _, k, n = pieces[u]
            return stage[:, u % 3, 0:k * n].rearrange("p (k n) -> p k n", k=k)

        @block.sync
        def _(sp):
            def load_x(s):
                sp.dma_start(xs[:, 2 * s:2 * s + 2, :], x_t[:, 2 * s:2 * s + 2, :]).then_inc(x_in[s], 16)

            def load_w(u):
                sp.dma_start(staged(u), pieces[u][0]).then_inc(w_in[u], 16)

            load_w(0)
            load_x(0)
            load_x(1)
            load_w(1)
            load_w(2)
            sp.dma_start(q_raw[:, 0, :].rearrange("p (k n) -> p k n", k=KD),
                         q_fc.rearrange("(k p) n -> p k n", p=P)).then_inc(q_in, 16)
            sp.dma_start(q_raw[:, 1, :].rearrange("p (k n) -> p k n", k=KH),
                         q_proj.rearrange("(k p) n -> p k n", p=P)).then_inc(q_in, 16)
            sp.wait_ge(w_lo, 1)
            load_w(3)
            sp.wait_ge(w_lo, 2)
            load_w(4)
            load_x(2)
            load_x(3)
            sp.wait_ge(w_lo, 3)
            load_w(5)
            sp.wait_ge(w_lo_pool, 1)
            load_w(6)
            sp.wait_ge(w_lo_pool, 2)
            load_w(7)
            for t in range(NT):
                if t < NT - 1:
                    sp.wait_ge(out_ready, t + 1)
                else:
                    sp.wait_ge(last_ready, 1)
                sp.dma_start(out_t[:, t, :], xs[:, t, :]).then_inc(stored, 16)
            sp.wait_ge(stored, 16 * NT)

        @block.tensor
        def _(pe):
            def take(*name):
                if USE[name] > 0:
                    pe.wait_ge(bank_read[BANK[name]], USE[name])
                return banks[BANK[name]]

            def product(dst, lhs, rhs, n, start=True):
                steps = [(a, c, k) for k in range(n) for a, c in ((0, 0), (0, 1), (1, 0))]
                for i, (a, c, k) in enumerate(steps):
                    last = nc.tensor.matmul(dst, lhs(k)[a], rhs(k)[c], start=start and i == 0,
                                            stop=i == len(steps) - 1)
                return last

            def feat(k, c0=0, n=HALF):
                return feat_hi[:, k, c0:c0 + n], feat_lo[:, k, c0:c0 + n]

            def transposes(name, src, t0, ready=lambda j: None):
                dst = take(*name)
                for j in range(2):
                    ready(j)
                    for k in range(KD):
                        last = nc.tensor.transpose(dst[:, k * SL + j * P:k * SL + (j + 1) * P],
                                                   src[:, t0 + j, k * P:(k + 1) * P], ident[:])
                last.then_inc(psum_filled, 1)

            def warm_up(n):
                for _ in range(n):
                    nc.tensor.matmul(ybank[0][:], warm[:, 0:P], warm[:], start=True, stop=True)

            def x_transposes(h, b):
                if h == 0 and b == 0:
                    pe.wait_ge(consts, 1)
                transposes(("T", h, b), xn[:, b, :, :], 0,
                           lambda j: pe.wait_ge(xn_ready, 2 * (2 * h + b) + j + 1))

            def token_major_x(h, b):
                if h == 0 and b == 0:
                    warm_up(3)
                wait_split(pe, "T", h, b)
                if h == 0 and b == 0:
                    pe.wait_ge(w_hi, 1)
                    pe.wait_ge(w_lo, 1)
                dst = take("XD", h, b)
                for j in range(2):
                    last = product(dst[:, j * XD:(j + 1) * XD], lambda k, c=(2 * b + j) * P: feat(k, c, P),
                                   lambda k: (wx_hi[:, k, 0:XD], wx_lo[:, k, 0:XD]), KD)
                last.then_inc(psum_filled, 1)

            def feature_major(name, hi, lo, c):
                product(take(*name)[:], lambda k: (hi[:, k, c:c + P], lo[:, k, c:c + P]), feat,
                        KD).then_inc(psum_filled, 1)

            def c_features(h, i):
                if h == 0 and i == 0:
                    pe.wait_ge(w_hi, 2)
                    pe.wait_ge(w_lo, 2)
                feature_major(("C", h, i), wc_hi, wc_lo, i * P)

            def z_features(h, i):
                if h == 0 and i == 0:
                    pe.wait_ge(w_hi, 3)
                    pe.wait_ge(w_lo, 3)
                feature_major(("Z", h, i), wz_hi, wz_lo, i * P)

            def mlp_up(h, m):
                if h == 0 and m == 0:
                    pe.wait_ge(w_hi, 5)
                    pe.wait_ge(w_lo_pool, 2)
                feature_major(("FC1", h, m), f1_hi, f1_lo, m * P)

            def weight_means():
                pe.wait_ge(absum_ready, 2)
                nc.tensor.matmul(take("AM")[:, 0:2], tri1[:, 1, :], absum[:], start=True, stop=True)\
                    .then_inc(psum_filled, 1)

            def sums_by_token(h):
                pe.wait_ge(dt_ready, h + 1)
                tri, one, da = tri1[:, 0, :], tri1[:, 1, :], dtw[:, 7, :, :]
                first, second = slice(0, TPH, 2), slice(1, TPH, 2)
                dst = take("CUMS", h)[:, 0:TPH * NH].rearrange("p (t n) -> p t n", t=TPH)
                nc.tensor.matmul(dst[:, first, :], tri, da[:, first, :], start=True, stop=True)
                nc.tensor.matmul(dst[:, second, :], one, da[:, first, :], start=True, stop=False)
                nc.tensor.matmul(dst[:, second, :], tri, da[:, second, :], start=False, stop=True)\
                    .then_inc(psum_filled, 1)

            def sums_by_head(h):
                da = dtw[:, 7, :, :]
                dst = take("CUMT", h)
                for b in range(2):
                    c = b * SL
                    nc.tensor.matmul(dst[0:NH, c:c + SL], da[:, 2 * b, :], tri1[:].rearrange("p a c -> p (a c)"),
                                     start=True, stop=False)
                    last = nc.tensor.matmul(dst[0:NH, c + P:c + SL], da[:, 2 * b + 1, :], tri1[:, 0, :],
                                            start=False, stop=True)
                last.then_inc(psum_filled, 1)

            def decay_sums(s, i):
                if s % 2 == 0 and i == 0:
                    wait_read(pe, "CUMT", s // 2)
                    if s == 0:
                        pe.wait_ge(sel_ready, 1)
                c0 = (s % 2) * SL
                dst = take("CB", s, i)
                for a in range(2):
                    last = nc.tensor.matmul(dst[:, a * SL:(a + 1) * SL], sel[:, a * REP + i, :],
                                            cumt[:, c0:c0 + SL], start=True, stop=True)
                last.then_inc(psum_filled, 1)

            def scores(s, i, a):
                c0 = (s % 2) * SL
                dst = take("G", s, i, a)
                for key in range(2):
                    keys = slice(c0 + key * P, c0 + (key + 1) * P)
                    queries = slice(c0 + key * P, c0 + SL)
                    place = slice(0, SL) if key == 0 else slice(SL, BLK)
                    nc.tensor.matmul(dst[:, place], b_hh[:, a, keys], c_hl[:, a, i, queries], start=True, stop=False)
                    last = nc.tensor.matmul(dst[:, place], b_ll[:, a, keys], c_hl[:, a, i, queries],
                                            start=False, stop=True)
                last.then_inc(psum_filled, 1)

            def scan(s, i):
                n = s * PAIRS + i
                pe.wait_ge(masked, n + 1)
                if i == 0:
                    pe.wait_ge(xdt_ready, s + 1)
                if i % 2 == 0 and s > 0:
                    pe.wait_ge(y_read, 2 * s + i // 2 - 1)
                for a in range(2):
                    e = decay[:, n % ESLOTS, a, :]
                    head = slice((a * REP + i) * HD, (a * REP + i + 1) * HD)
                    dst = ybank[i // 2][a * HD:(a + 1) * HD, (i % 2) * SL:(i % 2 + 1) * SL]
                    nc.tensor.matmul(dst, xdt[:, 0, head], e[:, 0:SL], start=True, stop=False)
                    last = nc.tensor.matmul(dst[:, P:SL], xdt[:, 1, head], e[:, SL:BLK], start=False, stop=True)
                last.then_inc(y_summed, 1)

            def mlp_down(s, j):
                if s == 0 and j == 0:
                    pe.wait_ge(w_hi, 7)
                    pe.wait_ge(w_lo_pool, 4)
                if j == 0 and s % 2 == 0:
                    for m in (KF - 2, KF - 1):
                        wait_split(pe, "FC1", s // 2, m)
                c = ((s % 2) * 2 + j) * P
                dst = (take("DOWN", s) if j == 0 else bank("DOWN", s))[:, j * D:(j + 1) * D]
                last = product(dst, lambda k: (g_hi[:, k, c:c + P], g_lo[:, k, c:c + P]),
                               lambda k: (f2_hi[:, k, :], f2_lo[:, k, :]), KF)
                if j == 1:
                    last.then_inc(psum_filled, 1)

            def out_projection(s, j):
                if s == 0 and j == 0:
                    pe.wait_ge(w_hi, 8)
                    pe.wait_ge(w_lo, 4)
                if j == 0:
                    pe.wait_ge(yt_ready, 2 * s + 2)
                dst = take("OUT", s) if j == 0 else bank("OUT", s)
                last = product(dst[:, j * D:(j + 1) * D],
                               lambda k: (yt_hi[:, k, j * P:(j + 1) * P], yt_lo[:, k, j * P:(j + 1) * P]),
                               lambda k: (wo_hi[:, k, :], wo_lo[:, k, :]), KI)
                if j == 1:
                    last.then_inc(psum_filled, 1)

            def square_sums(s):
                pe.wait_ge(sqs_ready, 3 * s + 3)
                dst = take("SS", s)
                for j in range(2):
                    last = nc.tensor.matmul(dst[:, 2 * j:2 * j + 2], sq[:, 0, j * P:(j + 1) * P], tri1[:, 1, 0:2],
                                            start=True, stop=True)
                last.then_inc(psum_filled, 1)

            def x1_transposes(s):
                pe.wait_ge(x1_ready, s + 1)
                transposes(("X1T", s), xs, 2 * s)

            def ternary_up(s, m2):
                if m2 == 0:
                    wait_read(pe, "X1T", s)
                    if s == 0:
                        pe.wait_ge(q_ready, 2)
                dst = take("FF1", s, m2)
                c = (s % 2) * SL
                for m in range(2 * m2, min(2 * m2 + 2, KH)):
                    for n in range(2 * KD):
                        last = nc.tensor.matmul(dst[:, (m % 2) * SL:(m % 2 + 1) * SL], q1[:, n // 2, m * P:(m + 1) * P],
                                                feat(n // 2, c, SL)[n % 2], start=n == 0, stop=n == 2 * KD - 1)
                last.then_inc(psum_filled, 1)

            def ternary_down(s, j):
                dst = take("FF2", s, j)
                for m in range(KH):
                    if j == 0 and m % 2 == 0:
                        wait_split(pe, "FF1", s, m // 2)
                    for n, h in enumerate((h_hi, h_lo)):
                        last = nc.tensor.matmul(dst[:, 0:D], h[:, s % 2, m, j * P:(j + 1) * P], q2[:, m, :],
                                                start=m == 0 and n == 0, stop=m == KH - 1 and n == 1)
                last.then_inc(psum_filled, 1)

            stages = {
                "T": x_transposes, "XD": token_major_x, "C": c_features, "Z": z_features, "FC1": mlp_up,
                "XT": lambda h: feature_major(("XT", h), wx_hi, wx_lo, 0),
                "BT": lambda h: feature_major(("BT", h), wx_hi, wx_lo, XD),
                "AM": weight_means, "CUMS": sums_by_token, "CUMT": sums_by_head, "CB": decay_sums,
                "G": scores, "SCAN": scan,
                "DOWN": mlp_down, "OUT": out_projection, "SS": square_sums, "X1T": x1_transposes,
                "FF1": ternary_up, "FF2": ternary_down,
            }
            pe.wait_ge(warm_ready, 1)
            warm_up(14)
            for step in tensor_order():
                stages[step[0]](*step[1:])

        @block.scalar
        def _(act):
            def weight_hi(u):
                act.wait_ge(w_in[u], 16)
                if u == 7:
                    for k in range(KI):
                        last = nc.scalar.activation(piece_hi[u][:, k, :], staged(u)[:, k, :], ACT.Copy,
                                                    scale=colv[:, NW + k:NW + k + 1])
                else:
                    last = nc.scalar.activation(piece_hi[u], staged(u), ACT.Copy)
                last.then_inc(w_hi, 1)

            def f_slot(*name):
                n = FUSE[name]
                if n >= FSLOTS:
                    wait_split(act, *f_uses[n - FSLOTS])
                return ftmp[:, n % FSLOTS, :]

            def features(h, b):
                wait_filled(act, "T", h, b)
                f = f_slot("T", h, b)
                src = bank("T", h, b)
                for k in range(KD):
                    last = nc.scalar.activation(f[:, k * SL:(k + 1) * SL], src[:, k * SL:(k + 1) * SL], ACT.Identity,
                                                scale=colv[:, LNW + k:LNW + k + 1], bias=colv[:, LNB + k:LNB + k + 1])
                last.then_inc(done_with("T", h, b), 1)

            def token_major_x(h, b):
                wait_filled(act, "XD", h, b)
                nc.scalar.activation(xd[:, 2 * b:2 * b + 2, :],
                                     bank("XD", h, b)[:, 0:2 * XD].rearrange("p (t n) -> p t n", t=2),
                                     ACT.Copy).then_inc(done_with("XD", h, b), 1)

            def x_features(h):
                wait_filled(act, "XT", h)
                nc.scalar.activation(xt[:], bank("XT", h)[:], ACT.Copy).then_inc(done_with("XT", h), 1)

            def b_features(h):
                wait_filled(act, "BT", h)
                for g in range(GROUPS):
                    for half in range(2):
                        last = nc.scalar.activation(b_hh[half * HD:(half + 1) * HD, g, :],
                                                    bank("BT", h)[g * HD:(g + 1) * HD, :], ACT.Copy)
                last.then_inc(hi_taken, 1)

            def c_features(h, i):
                wait_filled(act, "C", h, i)
                for g in range(GROUPS):
                    last = nc.scalar.activation(c_hl[0:HD, g, i, :], bank("C", h, i)[g * HD:(g + 1) * HD, :], ACT.Copy)
                last.then_inc(hi_taken, 1)

            def step_exponentials(h):
                act.wait_ge(u_abs, h + 1)
                nc.scalar.activation(dtw[:, 2, :, :], dtw[:, 1, :, :], ACT.Exp, scale=-1.0).then_inc(u_exp, 1)

            def gates(h, i):
                wait_filled(act, "Z", h, i)
                nc.scalar.activation(zs[:, i, :], bank("Z", h, i)[:], ACT.Silu).then_inc(done_with("Z", h, i), 1)

            def gelu(h, m):
                wait_filled(act, "FC1", h, m)
                nc.scalar.activation(f_slot("FC1", h, m), bank("FC1", h, m)[:], ACT.Gelu_apprx_tanh,
                                     bias=colv[:, FB1 + m:FB1 + m + 1]).then_inc(done_with("FC1", h, m), 1)

            def sums_out(h):
                wait_filled(act, "CUMS", h)
                nc.scalar.activation(cums[:], bank("CUMS", h)[:, 0:TPH * NH].rearrange("p (t n) -> p t n", t=TPH),
                                     ACT.Copy).then_inc(done_with("CUMS", h), 1)
                wait_filled(act, "CUMT", h)
                nc.scalar.activation(cumt[0:NH, :], bank("CUMT", h)[0:NH, :], ACT.Copy).then_inc(hi_taken, 1)

            def decays(s, i):
                n = s * PAIRS + i
                t0 = (s % 2) * 2
                if n == 0:
                    act.wait_ge(q_ready, 2)
                if s % 2 == 0 and i == 0:
                    wait_read(act, "CUMS", s // 2)
                if n >= ESLOTS:
                    act.wait_ge(y_summed, n - ESLOTS + 1)
                wait_filled(act, "CB", s, i)
                src = bank("CB", s, i)
                for a in range(2):
                    head = a * REP + i
                    e = decay[:, n % ESLOTS, a, :]
                    nc.scalar.activation(e[:, 0:SL], src[:, a * SL:(a + 1) * SL], ACT.Exp, scale=-1.0,
                                         bias=cums[:, t0, head:head + 1])
                    last = nc.scalar.activation(e[:, SL:BLK], src[:, a * SL + P:(a + 1) * SL], ACT.Exp, scale=-1.0,
                                                bias=cums[:, t0 + 1, head:head + 1])
                last.then_inc(done_with("CB", s, i), 1)

            def squares(s, k):
                act.wait_ge(yg_ready, 2 * s + k + 1)
                if s > 0:
                    wait_filled(act, "SS", s - 1)
                nc.scalar.activation(sq[:, 2 * k:2 * k + 2, :], yb[:, 2 * k:2 * k + 2, :], ACT.Square)\
                    .then_inc(sq_ready, 1)

            def mean_squares(s):
                wait_filled(act, "SS", s)
                nc.scalar.activation(mse[:, s, :], bank("SS", s)[:, 0:4:2], ACT.Copy, scale=1.0 / DI, bias=EPS)\
                    .then_inc(done_with("SS", s), 1)

            def x1_features(s):
                wait_filled(act, "X1T", s)
                c = (s % 2) * SL
                nc.scalar.activation(feat_hi[:, :, c:c + SL], bank("X1T", s)[:].rearrange("p (k t) -> p k t", k=KD),
                                     ACT.Copy).then_inc(hi_taken, 1)

            def squared_relus(s):
                for m2 in range(HP):
                    name = ("FF1", s, m2)
                    wait_filled(act, *name)
                    w = SL * min(2, KH - 2 * m2)
                    f = f_slot(*name)[:, 0:w]
                    nc.scalar.activation(f, bank(*name)[:, 0:w], ACT.Relu).then_inc(done_with(*name), 1)
                    wait_read(act, *name)
                    nc.scalar.activation(f, f, ACT.Square).then_inc(h_ready, 1)

            def outputs(s):
                act.wait_ge(mean_scaled, 2 * s + 2)
                for t in range(2 * s, min(2 * s + 2, NT - 1)):
                    nc.scalar.activation(xs[:, t, :], xs[:, t, :], ACT.Identity, scale=rstd[:, t:t + 1],
                                         bias=shift[:, t:t + 1]).then_inc(out_ready, 1)

            def weight_sums():
                act.wait_ge(q_in, 32)
                for n in range(2):
                    if n > 0:
                        act.wait_ge(absum_ready, n)
                    nc.scalar.activation(q_below[:], q_raw[:, n, :], ACT.Abs, accum_out=absum[:, n:n + 1])\
                        .then_inc(absum_ready, 1)

            act.dma_start(colv[:], cols).then_inc(vec_in, 16)
            act.dma_start(rowv[:], rows.broadcast_to([P, 2 * NH])).then_inc(vec_in, 16)
            act.dma_start(b2_half[:], b2.broadcast_to([P, D])).then_inc(b2_in, 16)
            weight_hi(0)
            act.wait_ge(vec_in, 32)
            nc.scalar.activation(expa[:], rowv[:, NH:2 * NH], ACT.Exp).then_inc(expa_ready, 1)
            weight_hi(1)
            features(0, 0)
            features(0, 1)
            weight_hi(2)
            weight_sums()
            token_major_x(0, 0)
            token_major_x(0, 1)
            weight_hi(3)
            b_features(0)
            x_features(0)
            weight_hi(4)
            c_features(0, 0)
            for h in range(2):
                s0, s1 = 2 * h, 2 * h + 1
                c_features(h, 1)
                if h == 0:
                    step_exponentials(0)
                    weight_hi(5)
                if h == 1:
                    x_features(1)
                c_features(h, 2)
                c_features(h, 3)
                gates(h, 3)
                if h == 0:
                    weight_hi(6)
                gates(h, 2)
                gates(h, 1)
                gates(h, 0)
                gelu(h, 0)
                gelu(h, 1)
                if h == 0:
                    weight_hi(7)
                gelu(h, 2)
                sums_out(h)
                gelu(h, 3)
                gelu(h, 4)
                gelu(h, 5)
                decays(s0, 0)
                decays(s0, 1)
                decays(s0, 2)
                decays(s0, 3)
                gelu(h, 6)
                gelu(h, 7)
                decays(s1, 1)
                decays(s1, 0)
                squares(s0, 0)
                decays(s1, 2)
                squares(s0, 1)
                mean_squares(s0)
                decays(s1, 3)
                if h == 0:
                    features(1, 0)
                    features(1, 1)
                    squares(1, 0)
                    squares(1, 1)
                    token_major_x(1, 1)
                    b_features(1)
                    token_major_x(1, 0)
                    mean_squares(1)
                    c_features(1, 0)
                    step_exponentials(1)
                else:
                    x1_features(0)
                    squares(3, 0)
                    squares(3, 1)
                    squared_relus(0)
                    mean_squares(3)
                    x1_features(1)
                    x1_features(2)
                    squared_relus(1)
            x1_features(3)
            squared_relus(2)
            squared_relus(3)
            outputs(0)
            outputs(1)
            outputs(2)
            outputs(3)

        @block.vector
        def _(dve):
            steps = [0]

            def mark(ins):
                ins.then_inc(dve_step, 1)
                steps[0] += 1
                return steps[0]

            def link(ins):
                dve.wait_ge(dve_step, mark(ins))

            def statistics(tiles):
                marks = [mark(nc.vector.bn_stats(st[:, t, :], xs[:, t, :])) for t in tiles]
                for t, m in zip(tiles, marks):
                    dve.wait_ge(dve_step, m)
                    last = nc.vector.bn_aggr(mv[:, t, :], st[:, t, :])
                    last.then_inc(var_ready, 1)

            def normalise(t, dst):
                return nc.vector.tensor_scalar(dst, xs[:, t, :], mv[:, t, 0:1], rstd[:, t:t + 1],
                                               ALU.subtract, ALU.mult)

            def first_norm_statistics(s):
                dve.wait_ge(x_in[s], 16)
                statistics((2 * s, 2 * s + 1))

            def first_norm(s):
                dve.wait_ge(rstd_ready, s + 1)
                if s >= 2:
                    wait_filled(dve, "T", 0, s - 2)
                for j in range(2):
                    normalise(2 * s + j, xn[:, s % 2, j, :]).then_inc(xn_ready, 1)

            def weight_lo(u):
                dve.wait_ge(w_hi, u + 1)
                if u == 7:
                    for k in range(KI):
                        last = nc.vector.scalar_tensor_tensor(piece_lo[u][:, k, :], staged(u)[:, k, :],
                                                              colv[:, NW + k:NW + k + 1],
                                                              piece_hi[u][:, k, :].bitcast(f32), ALU.mult,
                                                              ALU.subtract)
                else:
                    last = nc.vector.tensor_tensor(piece_lo[u], staged(u), piece_hi[u].bitcast(f32), ALU.subtract)
                last.then_inc(w_lo, 1)

            def split_f(hi, lo, f):
                link(nc.vector.tensor_copy(hi, f))
                nc.vector.tensor_tensor(lo, f, hi.bitcast(f32), ALU.subtract).then_inc(f_split, 1)

            def f_of(*name):
                return ftmp[:, FUSE[name] % FSLOTS, :]

            def features(h, b):
                wait_read(dve, "T", h, b)
                c = slice(b * SL, (b + 1) * SL)
                split_f(feat_hi[:, :, c], feat_lo[:, :, c],
                        f_of("T", h, b).rearrange("p (k t) -> p k t", k=KD))

            def step_inputs(h):
                for b in range(2):
                    wait_read(dve, "XD", h, b)
                if h == 0:
                    dve.wait_ge(vec_in, 32)
                link(nc.vector.tensor_tensor(dtw[:, 0, :, :], xd[:, :, XD - NH:XD],
                                             rowv[:, 0:NH].unsqueeze(1).broadcast_to([P, TPH, NH]), ALU.add))
                nc.vector.scalar_tensor_tensor(dtw[:, 1, :, :], dtw[:, 0, :, :], -1.0, dtw[:, 0, :, :], ALU.mult,
                                               ALU.max).then_inc(u_abs, 1)

            def step_sizes(h):
                dve.wait_ge(u_exp, h + 1)
                u, e, r, s, s2, q, dt, da = (dtw[:, n, :, :] for n in (0, 2, 3, 4, 5, 3, 6, 7))
                link(nc.vector.tensor_scalar(r, e, 2.0, None, ALU.add))
                link(nc.vector.reciprocal(s2, r))
                link(nc.vector.tensor_tensor(s, e, s2, ALU.mult))
                link(nc.vector.tensor_tensor(s2, s, s, ALU.mult))
                link(nc.vector.tensor_scalar(q, s2, 1.0 / 17, None, ALU.mult))
                for n in (15, 13, 11, 9, 7, 5, 3):
                    link(nc.vector.scalar_tensor_tensor(q, q, 1.0 / n, s2, ALU.add, ALU.mult))
                link(nc.vector.scalar_tensor_tensor(q, q, 1.0, s, ALU.add, ALU.mult))
                link(nc.vector.tensor_scalar(s, u, 0.0, None, ALU.max))
                link(nc.vector.scalar_tensor_tensor(dt, q, 2.0, s, ALU.mult, ALU.add))
                if h == 0:
                    dve.wait_ge(expa_ready, 1)
                nc.vector.tensor_tensor(da, dt, expa[:].unsqueeze(1).broadcast_to([P, TPH, NH]), ALU.mult)\
                    .then_inc(dt_ready, 1)

            def b_features(h):
                dve.wait_ge(hi_taken, HI[("BT", h)])
                for g in range(GROUPS):
                    for half in range(2):
                        r = slice(half * HD, (half + 1) * HD)
                        last = nc.vector.tensor_tensor(b_ll[r, g, :], bank("BT", h)[g * HD:(g + 1) * HD, :],
                                                       b_hh[r, g, :].bitcast(f32), ALU.subtract)
                last.then_inc(done_with("BT", h), 1)

            def c_features(h, i):
                dve.wait_ge(hi_taken, HI[("C", h, i)])
                for g in range(GROUPS):
                    last = nc.vector.tensor_tensor(c_hl[HD:P, g, i, :], bank("C", h, i)[g * HD:(g + 1) * HD, :],
                                                   c_hl[0:HD, g, i, :].bitcast(f32), ALU.subtract)
                last.then_inc(done_with("C", h, i), 1)

            def ternary_means():
                wait_filled(dve, "AM")
                link(nc.vector.tensor_scalar(am[:], bank("AM")[:, 0:2], 1.0 / (D * H2), 1e-5, ALU.mult, ALU.max))
                nc.vector.tensor_tensor(am11[:], am[:, 0:1], am[:, 0:1], ALU.mult).then_inc(done_with("AM"), 1)
                mark(nc.vector.tensor_scalar(thr[:, 0, :], am[:], 0.7, None, ALU.mult))
                link(nc.vector.tensor_scalar(thr[:, 1, :], am[:], -0.7, None, ALU.mult))
                mark(nc.vector.tensor_tensor(qscale[:], am11[:], am[:, 1:2], ALU.mult))

            def ternary_weights(n):
                if n > 0:
                    dve.wait_ge(q_ready, n)
                link(nc.vector.tensor_scalar(q_below[:], q_raw[:, n, :], thr[:, 1, n:n + 1], None, ALU.is_lt))
                nc.vector.scalar_tensor_tensor((q1, q2)[n][:].rearrange("p k n -> p (k n)"), q_raw[:, n, :],
                                               thr[:, 0, n:n + 1], q_below[:], ALU.is_gt, ALU.subtract)\
                    .then_inc(q_ready, 1)

            def gelu_parts(h, m):
                wait_read(dve, "FC1", h, m)
                if m in ON_VECTOR:
                    split_f(g_hi[:, m, :], g_lo[:, m, :], f_of("FC1", h, m))
                else:
                    nc.vector.tensor_copy(g_hi[:, m, :], f_of("FC1", h, m)).then_inc(g_copied, 1)

            def sums_out(h):
                dve.wait_ge(hi_taken, HI[("CUMT", h)])
                nc.vector.tensor_tensor(cumt[32:32 + NH, :], bank("CUMT", h)[0:NH, :], cumt[0:NH, :].bitcast(f32),
                                        ALU.subtract).then_inc(done_with("CUMT", h), 1)

            def weighted_scores(s, i):
                n = s * PAIRS + i
                wait_read(dve, "CB", s, i)
                for a in range(2):
                    wait_filled(dve, "G", s, i, a)
                    e = decay[:, n % ESLOTS, a, :]
                    nc.vector.tensor_tensor(e, bank("G", s, i, a)[:, 0:BLK], e, ALU.mult)\
                        .then_inc(done_with("G", s, i, a), 1)

            def gated(s, k):
                tokens = slice((s % 2) * SL, (s % 2 + 1) * SL)
                pairs = slice(2 * k, 2 * k + 2)
                dve.wait_ge(y_summed, s * PAIRS + 2 * k + 2)
                if s > 0:
                    dve.wait_ge(sq_ready, 2 * s + k - 1)
                for i in (2 * k, 2 * k + 1):
                    last = nc.vector.scalar_tensor_tensor(yb[:, i, :], xt[:, tokens], colv[:, DV + i:DV + i + 1],
                                                          ybank[k][:, (i % 2) * SL:(i % 2 + 1) * SL],
                                                          ALU.mult, ALU.add)
                last.then_inc(y_read, 1)
                dve.wait_ge(y_read, 2 * s + k + 1)
                nc.vector.tensor_tensor(yb[:, pairs, :], yb[:, pairs, :], zs[:, pairs, tokens], ALU.mult)\
                    .then_inc(yg_ready, 1)
                dve.wait_ge(yg_ready, 2 * s + k + 1)
                if s > 0:
                    wait_filled(dve, "OUT", s - 1)
                nc.vector.tensor_copy(yt_hi[:, pairs, :], yb[:, pairs, :]).then_inc(yt_copied, 1)
                dve.wait_ge(yt_copied, 2 * s + k + 1)
                nc.vector.tensor_tensor(yt_lo[:, pairs, :], yb[:, pairs, :], yt_hi[:, pairs, :].bitcast(f32),
                                        ALU.subtract).then_inc(yt_ready, 1)

            def residual(s):
                dve.wait_ge(biased, s + 1)
                wait_filled(dve, "DOWN", s)
                x_tiles = xs[:, 2 * s:2 * s + 2, :]
                nc.vector.scalar_tensor_tensor(x_tiles, x_tiles, 2.0,
                                               bank("DOWN", s)[:].rearrange("p (t d) -> p t d", t=2),
                                               ALU.mult, ALU.add).then_inc(done_with("DOWN", s), 1)

            def joined(s):
                dve.wait_ge(rsy_ready, s + 1)
                wait_read(dve, "DOWN", s)
                wait_filled(dve, "OUT", s)
                for j in range(2):
                    t = 2 * s + j
                    last = nc.vector.scalar_tensor_tensor(xs[:, t, :], bank("OUT", s)[:, j * D:(j + 1) * D],
                                                          rsy[:, t:t + 1], xs[:, t, :], ALU.mult, ALU.add)
                last.then_inc(done_with("OUT", s), 1)

            def second_norm_statistics(s):
                wait_read(dve, "OUT", s)
                statistics((2 * s, 2 * s + 1))

            def second_norm(s):
                dve.wait_ge(rstd_ready, NORMS.index(("second", s)) + 1)
                for j in range(2):
                    last = normalise(2 * s + j, xs[:, 2 * s + j, :])
                last.then_inc(x1_ready, 1)

            def x1_features(s):
                dve.wait_ge(hi_taken, HI[("X1T", s)])
                c = (s % 2) * SL
                nc.vector.tensor_tensor(feat_lo[:, :, c:c + SL], bank("X1T", s)[:].rearrange("p (k t) -> p k t", k=KD),
                                        feat_hi[:, :, c:c + SL].bitcast(f32), ALU.subtract)\
                    .then_inc(done_with("X1T", s), 1)

            def squared_parts(s):
                if s >= 2:
                    wait_filled(dve, "FF2", s - 2, 1)
                for m2 in range(HP):
                    dve.wait_ge(h_ready, s * HP + m2 + 1)
                    m = slice(2 * m2, min(2 * m2 + 2, KH))
                    w = SL * (m.stop - m.start)
                    split_f(h_hi[:, s % 2, m, :], h_lo[:, s % 2, m, :],
                            f_of("FF1", s, m2)[:, 0:w].rearrange("p (k t) -> p k t", t=SL))

            def output_sum(s, j):
                t = 2 * s + j
                wait_filled(dve, "FF2", s, j)
                if j == 0:
                    dve.wait_ge(x1_ready, s + 1)
                nc.vector.scalar_tensor_tensor(xs[:, t, :], bank("FF2", s, j)[:, 0:D], qscale[:],
                                               xs[:, t, :], ALU.mult, ALU.add).then_inc(done_with("FF2", s, j), 1)

            def third_norm_statistics(s, j):
                wait_read(dve, "FF2", s, j)
                statistics((2 * s + j,))

            def output_sums(s):
                for j in range(2):
                    output_sum(s, j)
                    third_norm_statistics(s, j)

            def last_output():
                dve.wait_ge(rstd_ready, NORMS.index(("third", SEQS - 1)) + 1)
                normalise(NT - 1, xs[:, NT - 1, :]).then_inc(last_ready, 1)

            first_norm_statistics(0)
            first_norm_statistics(1)
            first_norm(0)
            weight_lo(0)
            first_norm(1)
            features(0, 0)
            features(0, 1)
            weight_lo(1)
            dve.wait_ge(consts, 1)
            nc.vector.tensor_copy(sel[:], sel_f[:].unsqueeze(2).broadcast_to([40, NH, P])).then_inc(sel_ready, 1)
            weight_lo(2)
            step_inputs(0)
            ternary_means()
            ternary_weights(0)
            b_features(0)
            c_features(0, 0)
            for h in range(2):
                s0, s1 = 2 * h, 2 * h + 1
                c_features(h, 1)
                c_features(h, 2)
                c_features(h, 3)
                if h == 1:
                    second_norm(1)
                step_sizes(h)
                if h == 0:
                    ternary_weights(1)
                gelu_parts(h, 0)
                gelu_parts(h, 1)
                gelu_parts(h, 2)
                sums_out(h)
                if h == 0:
                    weight_lo(7)
                gelu_parts(h, 3)
                gelu_parts(h, 5)
                gelu_parts(h, 4)
                weighted_scores(s0, 0)
                weighted_scores(s0, 1)
                if h == 0:
                    first_norm_statistics(2)
                    first_norm_statistics(3)
                weighted_scores(s0, 2)
                gelu_parts(h, 6)
                gelu_parts(h, 7)
                weighted_scores(s0, 3)
                gated(s0, 0)
                gated(s0, 1)
                weighted_scores(s1, 0)
                residual(s0)
                if h == 0:
                    first_norm(2)
                    first_norm(3)
                weighted_scores(s1, 1)
                joined(s0)
                weighted_scores(s1, 2)
                second_norm_statistics(s0)
                if h == 0:
                    features(1, 0)
                    features(1, 1)
                    weighted_scores(1, 3)
                    gated(1, 0)
                    second_norm(0)
                    gated(1, 1)
                    residual(1)
                    joined(1)
                    b_features(1)
                    step_inputs(1)
                    second_norm_statistics(1)
                    c_features(1, 0)
                else:
                    x1_features(0)
                    second_norm(2)
                    weighted_scores(3, 3)
                    gated(3, 0)
                    gated(3, 1)
                    residual(3)
                    squared_parts(0)
                    x1_features(1)
            joined(3)
            second_norm_statistics(3)
            x1_features(2)
            output_sum(0, 0)
            output_sum(0, 1)
            second_norm(3)
            squared_parts(1)
            third_norm_statistics(0, 0)
            third_norm_statistics(0, 1)
            output_sum(1, 0)
            x1_features(3)
            output_sum(1, 1)
            squared_parts(2)
            squared_parts(3)
            third_norm_statistics(1, 0)
            third_norm_statistics(1, 1)
            output_sums(2)
            output_sums(3)
            last_output()

        @block.gpsimd
        def _(pool):
            def rstd_of(kind, s):
                n = NORMS.index((kind, s))
                pool.wait_ge(var_ready, 2 * n + 2)
                nc.gpsimd.tensor_scalar(vare[:, n, :], mv[:, 2 * s:2 * s + 2, 1], EPS, None, ALU.add)\
                    .then_inc(eps_added, 1)
                pool.wait_ge(eps_added, n + 1)
                nc.gpsimd.tensor_tensor(rstd[:, 2 * s:2 * s + 2], vare[:, n, :], mhalf[:], ALU.pow)\
                    .then_inc(rstd_ready, 1)

            def third_norm(s):
                rstd_of("third", s)
                tiles = slice(2 * s, 2 * s + 2)
                nc.gpsimd.tensor_scalar(shift[:, tiles], mv[:, tiles, 0], -1.0, None, ALU.mult)\
                    .then_inc(mean_scaled, 1)
                pool.wait_ge(mean_scaled, 2 * s + 1)
                pool.wait_ge(rstd_ready, NORMS.index(("third", s)) + 1)
                nc.gpsimd.tensor_tensor(shift[:, tiles], shift[:, tiles], rstd[:, tiles], ALU.mult)\
                    .then_inc(mean_scaled, 1)

            def weight_lo(u):
                pool.wait_ge(w_hi, u + 1)
                nc.gpsimd.tensor_tensor(piece_lo[u], staged(u), piece_hi[u].bitcast(f32), ALU.subtract)\
                    .then_inc(w_lo_pool, 1)

            def gelu_lo(h, m):
                pool.wait_ge(g_copied, GELU_SPLITS.index((h, m)) + 1)
                nc.gpsimd.tensor_tensor(g_lo[:, m, :], ftmp[:, FUSE[("FC1", h, m)] % FSLOTS, :],
                                        g_hi[:, m, :].bitcast(f32), ALU.subtract).then_inc(g_split, 1)

            def stepped_x(s):
                if s == 0:
                    pool.wait_ge(w_lo, 4)
                if s % 2 == 0:
                    pool.wait_ge(dt_ready, s // 2 + 1)
                if s > 0:
                    pool.wait_ge(y_summed, s * PAIRS)
                for j in range(2):
                    t = (s % 2) * 2 + j
                    x_heads = xd[:, t, 0:GROUPS * HD].rearrange("p (g d) -> p g d", g=GROUPS)\
                        .unsqueeze(2).broadcast_to([P, GROUPS, REP, HD])
                    dt_heads = dtw[:, 6, t, :].rearrange("p (g r) -> p g r", g=GROUPS)\
                        .unsqueeze(3).broadcast_to([P, GROUPS, REP, HD])
                    last = nc.gpsimd.tensor_tensor(xdt[:, j, :].rearrange("p (g r d) -> p g r d", g=GROUPS, r=REP),
                                                   x_heads, dt_heads, ALU.mult)
                last.then_inc(xdt_ready, 1)

            def mask(s, i):
                n = s * PAIRS + i
                for a in range(2):
                    wait_read(pool, "G", s, i, a)
                    e = decay[:, n % ESLOTS, a, :].rearrange("p (k t) -> p k t", t=P)[:, 0:3:2, :]
                    last = nc.gpsimd.affine_select(out=e, in_=e, compare_op=ALU.is_ge, fill=0.0, base=0,
                                                   pattern=[[0, 2], [1, P]], channel_multiplier=-1)
                last.then_inc(masked, 1)

            def squares(s, k):
                pool.wait_ge(sq_ready, 2 * s + k + 1)
                nc.gpsimd.tensor_tensor(sq[:, 2 * k, :], sq[:, 2 * k, :], sq[:, 2 * k + 1, :], ALU.add)\
                    .then_inc(sqs_ready, 1)
                if k == 1:
                    pool.wait_ge(sqs_ready, 3 * s + 2)
                    nc.gpsimd.tensor_tensor(sq[:, 0, :], sq[:, 0, :], sq[:, 2, :], ALU.add).then_inc(sqs_ready, 1)

            def bias(s):
                pool.wait_ge(xn_ready, 2 * s + 2)
                if s == 0:
                    pool.wait_ge(b2_ready, 1)
                x_tiles = xs[:, 2 * s:2 * s + 2, :]
                nc.gpsimd.tensor_tensor(x_tiles, x_tiles, b2_half[:].unsqueeze(1).broadcast_to([P, 2, D]), ALU.add)\
                    .then_inc(biased, 1)

            def mixer_scale(s):
                wait_read(pool, "SS", s)
                nc.gpsimd.tensor_tensor(rsy[:, 2 * s:2 * s + 2], mse[:, s, :], mhalf[:], ALU.pow).then_inc(rsy_ready, 1)

            nc.gpsimd.memset(warm[:], 1.0).then_inc(warm_ready, 1)
            nc.gpsimd.memset(mhalf[:], -0.5)
            nc.gpsimd.memset(ident[:], 0.0).then_inc(zeroed, 1)
            nc.gpsimd.memset(tri1[:], 1.0).then_inc(zeroed, 1)
            nc.gpsimd.memset(sel_f[:], 0.0).then_inc(zeroed, 1)
            nc.gpsimd.memset(cumt[:].bitcast(f32), 0.0).then_inc(zeroed, 1)
            pool.wait_ge(zeroed, 4)
            nc.gpsimd.affine_select(out=ident[:], in_=ident[:], compare_op=ALU.not_equal, fill=1.0, base=0,
                                    pattern=[[-1, P]], channel_multiplier=1)
            nc.gpsimd.affine_select(out=tri1[:, 0, :], in_=tri1[:, 0, :], compare_op=ALU.is_ge, fill=0.0, base=0,
                                    pattern=[[1, P]], channel_multiplier=-1)
            nc.gpsimd.affine_select(out=sel_f[:], in_=sel_f[:], compare_op=ALU.not_equal, fill=1.0, base=0,
                                    pattern=[[-1, NH]], channel_multiplier=1).then_inc(zeroed, 1)
            pool.wait_ge(zeroed, 5)
            nc.gpsimd.affine_select(out=sel_f[:], in_=sel_f[:], compare_op=ALU.not_equal, fill=1.0, base=-32,
                                    pattern=[[-1, NH]], channel_multiplier=1).then_inc(consts, 1)
            rstd_of("first", 0)
            rstd_of("first", 1)
            pool.wait_ge(b2_in, 16)
            nc.gpsimd.tensor_scalar(b2_half[:], b2_half[:], 0.5, None, ALU.mult).then_inc(b2_ready, 1)
            bias(0)
            bias(1)
            weight_lo(3)
            weight_lo(4)
            weight_lo(5)
            weight_lo(6)
            for h in range(2):
                s0, s1 = 2 * h, 2 * h + 1
                gelu_lo(h, 0)
                gelu_lo(h, 1)
                gelu_lo(h, 2)
                gelu_lo(h, 3)
                stepped_x(s0)
                mask(s0, 0)
                gelu_lo(h, 4)
                mask(s0, 1)
                mask(s0, 2)
                gelu_lo(h, 6)
                mask(s0, 3)
                if h == 0:
                    rstd_of("first", 2)
                    rstd_of("first", 3)
                stepped_x(s1)
                squares(s0, 0)
                squares(s0, 1)
                mask(s1, 0)
                mixer_scale(s0)
                if h == 0:
                    bias(3)
                    bias(2)
                mask(s1, 1)
                rstd_of("second", s0)
                mask(s1, 2)
                mask(s1, 3)
                squares(s1, 0)
                squares(s1, 1)
                mixer_scale(s1)
                rstd_of("second", s1)
            third_norm(0)
            third_norm(1)
            third_norm(2)
            third_norm(3)


def kernel(**inputs):
    import numpy as np
    import concourse.bacc as bacc
    from concourse.bass_utils import run_bass_kernel_spmd

    a = {n.removeprefix("L0_"): np.asarray(v) for n, v in inputs.items()}
    w = a["attn_W_in"]
    xb0, b0, c0, dt0 = DI, DI + P, DI + 2 * P, 2 * DI + 2 * P

    def paired(m):
        return m.reshape(-1, GROUPS, REP, HD).transpose(0, 2, 1, 3).reshape(-1, DI)

    arrays = {
        "x": a["attn_hidden_states"].reshape(T, D),
        "w_xdb": np.concatenate([w[:, xb0:xb0 + P], w[:, dt0:dt0 + NH], w[:, b0:b0 + P]], axis=1),
        "w_c": paired(w[:, c0:c0 + DI]),
        "w_z": paired(w[:, 0:DI]),
        "fc1": a["attn_fc1_w"],
        "fc2": a["attn_fc2_w"],
        "w_out": paired(a["attn_W_out"].T).T,
        "q_fc": a["ffn_w_fc"].T,
        "q_proj": a["ffn_w_proj"].T,
        "cols": np.concatenate([v.reshape(-1, P).T for v in (
            a["attn_ln_w"], a["attn_ln_b"], a["attn_fc1_b"], paired(a["attn_norm_w"]),
            paired(np.repeat(a["attn_D"], HD)))], axis=1),
        "rows": np.concatenate([a["attn_dt_bias"], a["attn_A_log"]])[None, :],
        "b2": a["attn_fc2_b"][None, :],
    }
    arrays = {n: np.ascontiguousarray(v) for n, v in arrays.items()}
    nc = bacc.Bacc("TRN2", target_bir_lowering=False, num_devices=1)
    args = [nc.dram_tensor(n, v.shape, mybir.dt.from_np(v.dtype), kind="ExternalInput").ap() for n, v in arrays.items()]
    out = nc.dram_tensor("out", (T, D), mybir.dt.float32, kind="ExternalOutput").ap()
    block_kernel(nc, *args, out)
    result = run_bass_kernel_spmd(nc, [arrays], core_ids=[0])
    return result.results[0]["out"].reshape(SEQS, SL, D)
```
